# Optimizing a Trainium2 kernel written in Bass

```python
import numpy as np
import jax
import jax.numpy as jnp

def _softmax(x, axis=-1):
    return jax.nn.softmax(x, axis=axis)

def _gelu(x):
    return jax.nn.gelu(x, approximate=True)

def _silu(x):
    return jax.nn.silu(x)

def _sigmoid(x):
    return jax.nn.sigmoid(x)

def _layernorm(x, axis=-1, eps=1e-05):
    m = jnp.mean(x, axis=axis, keepdims=True)
    v = jnp.var(x, axis=axis, keepdims=True)
    return (x - m) / jnp.sqrt(v + eps)

def _scatter_add(tgt, idx, src, axis=0):
    return tgt.at[idx].add(src)

def _segment_sum(src, seg, n):
    return jax.ops.segment_sum(src, seg, n)
kernel_name = 'mk_pixart_resid_d4_seqx_r8_dfabfe'

def setup_inputs(seed: int=0):
    np.random.seed(seed)
    _w = jnp.asarray

    def _rec_inputs():
        import jax
        import jax.numpy as jnp
        _rk = jax.random.key(seed)
        x = 2.818e-05 + 1 * jax.random.normal(jax.random.fold_in(_rk, 1), (16, 128, 128), jnp.float32)
        _lenS = 128 - jax.random.randint(jax.random.fold_in(_rk, 7), (16,), 0, max(1, 128 // 4) + 1, jnp.int32)
        _lenS2 = 120 - jax.random.randint(jax.random.fold_in(_rk, 8), (16,), 0, max(1, 120 // 4) + 1, jnp.int32)
        _ctx_1024P = jax.random.normal(jax.random.fold_in(_rk, 11), (16, 16, 128), jnp.float32)
        _ctx_1024c = jax.random.dirichlet(jax.random.fold_in(_rk, 511), 0.3 * jnp.ones((16,), jnp.float32), (16, 120))
        _ctx_1024t = jnp.einsum('bsk,bkd->bsd', _ctx_1024c, _ctx_1024P)
        _ctx_1024t = _ctx_1024t * jax.lax.rsqrt(jnp.mean(jnp.square(_ctx_1024t)) + 1e-12) * 0.953939
        ctx_1024 = -0.000391444 + 0.999954 * (_ctx_1024t + 0.3 * jax.random.normal(jax.random.fold_in(_rk, 611), (16, 120, 128), jnp.float32))
        condB_pt = jax.random.uniform(jax.random.fold_in(_rk, 13), (16,), jnp.float32, 0.0, 226.919)
        condB_tau = jax.random.uniform(jax.random.fold_in(_rk, 14), (16,), jnp.float32, 0.0, 1.45372)
        fside_BxS2_0 = 0.0088954 + 1.00633 * jax.random.normal(jax.random.fold_in(_rk, 15), (16, 120), jnp.float32)
        return (x, ctx_1024, condB_pt, condB_tau, fside_BxS2_0, _lenS2)
    x, ctx_1024, condB_pt, condB_tau, fside_BxS2_0, _lenS2 = _rec_inputs()

    def _L0_xcond_setup():
        import jax, jax.numpy as jnp
        import numpy as np
        N, L, H, Q = (64, 258, 128, 32)
        WINDOW = 16.0
        DEV_POW = 128.0
        key = jax.random.key(seed)
        k1, k2, k3, k4, k5, k6 = jax.random.split(key, 6)
        encoder_outputs = jax.random.normal(k1, (N, L, H), dtype=jnp.float32)
        decoder_h_t = jax.random.normal(k2, (N, Q, H), dtype=jnp.float32)
        src_len = jax.random.randint(k3, (N,), 32, L + 1).astype(jnp.int32)
        p_t = jax.random.uniform(k4, (N,), dtype=jnp.float32) * (src_len.astype(jnp.float32) - 1.0)
        W_a = jax.random.normal(k5, (H, H), dtype=jnp.float32) * (1.0 / np.sqrt(H))
        W_c = jax.random.normal(k6, (H, 2 * H), dtype=jnp.float32) * (1.0 / np.sqrt(2 * H))
        return {'encoder_outputs': encoder_outputs, 'decoder_h_t': decoder_h_t, 'src_len': src_len, 'p_t': p_t, 'W_a': W_a, 'W_c': W_c}
    _L0_xcond_all = _L0_xcond_setup()
    _L0_xcond_in = {k: v for k, v in _L0_xcond_all.items() if k in ('W_a', 'W_c')}
    del _L0_xcond_all

    def _L0_ffn_setup():
        import jax, jax.numpy as jnp
        import numpy as np
        D = 128
        H = 512
        E = 8
        B = 2
        T = 256
        LN_EPS = 1e-05

        def _layer_norm(r, gamma, beta):
            mu = jnp.mean(r, axis=-1, keepdims=True)
            var = jnp.mean(jnp.square(r - mu), axis=-1, keepdims=True)
            return (r - mu) * jax.lax.rsqrt(var + LN_EPS) * gamma + beta
        key = jax.random.key(seed)
        ks = jax.random.split(key, 9)
        s_in = 1.0 / np.sqrt(D)
        s_hid = 1.0 / np.sqrt(H)
        x = jax.random.normal(ks[0], (B, T, D), dtype=jnp.float32)
        Wg = jax.random.uniform(ks[1], (D, E), jnp.float32, -s_in, s_in)
        bg = jax.random.uniform(ks[2], (E,), jnp.float32, -s_in, s_in)
        W1 = jax.random.uniform(ks[3], (E, D, H), jnp.float32, -s_in, s_in)
        b1 = jax.random.uniform(ks[4], (E, H), jnp.float32, -s_in, s_in)
        W2 = jax.random.uniform(ks[5], (E, H, D), jnp.float32, -s_hid, s_hid)
        b2 = jax.random.uniform(ks[6], (E, D), jnp.float32, -s_hid, s_hid)
        gamma = jnp.ones((D,), jnp.float32)
        beta = jnp.zeros((D,), jnp.float32)
        return {'x': x, 'Wg': Wg, 'bg': bg, 'W1': W1, 'b1': b1, 'W2': W2, 'b2': b2, 'gamma': gamma, 'beta': beta}
    _L0_ffn_all = _L0_ffn_setup()
    _L0_ffn_in = {k: v for k, v in _L0_ffn_all.items() if k in ('Wg', 'bg', 'W1', 'b1', 'W2', 'b2', 'gamma', 'beta')}
    del _L0_ffn_all

    def _L1_xcond_setup():
        import jax, jax.numpy as jnp
        import numpy as np
        D_MODEL = 128
        N_HEADS = 16
        key = jax.random.key(seed)
        ks = jax.random.split(key, 16)
        B, L, S, D = (4, 256, 256, D_MODEL)
        inp = {'q': jax.random.normal(ks[0], (B, L, D), jnp.float32), 'k': jax.random.normal(ks[1], (B, S, D), jnp.float32), 'v': jax.random.normal(ks[2], (B, S, D), jnp.float32), 'tau': jax.random.uniform(ks[3], (B, 1), jnp.float32, 0.5, 1.5), 'delta': jax.random.normal(ks[4], (B, S), jnp.float32)}
        s = 1.0 / np.sqrt(D)
        inp['Wq'] = jax.random.normal(ks[5], (D, D), jnp.float32) * s
        inp['bq'] = jnp.zeros((D,), jnp.float32)
        inp['Wk'] = jax.random.normal(ks[6], (D, D), jnp.float32) * s
        inp['bk'] = jnp.zeros((D,), jnp.float32)
        inp['Wv'] = jax.random.normal(ks[7], (D, D), jnp.float32) * s
        inp['bv'] = jnp.zeros((D,), jnp.float32)
        inp['Wo'] = jax.random.normal(ks[8], (D, D), jnp.float32) * s
        inp['bo'] = jnp.zeros((D,), jnp.float32)
        return inp
    _L1_xcond_all = _L1_xcond_setup()
    _L1_xcond_in = {k: v for k, v in _L1_xcond_all.items() if k in ('Wq', 'bq', 'Wk', 'bk', 'Wv', 'bv', 'Wo', 'bo')}
    del _L1_xcond_all

    def _L1_ffn_setup():
        import jax, jax.numpy as jnp
        import numpy as np
        DIM = 128
        MOE_HID = 64
        SHARED_HID = 256
        N_EXPERTS = 16
        TOP_K = 2
        NORM_TOPK_PROB = True
        key = jax.random.key(seed)
        ks = jax.random.split(key, 9)
        s = 0.02
        x = jax.random.normal(ks[0], (2, 128, DIM), dtype=jnp.float32)
        Wg = jax.random.normal(ks[1], (N_EXPERTS, DIM), dtype=jnp.float32) * s
        We_gate = jax.random.normal(ks[2], (N_EXPERTS, MOE_HID, DIM), dtype=jnp.float32) * s
        We_up = jax.random.normal(ks[3], (N_EXPERTS, MOE_HID, DIM), dtype=jnp.float32) * s
        We_down = jax.random.normal(ks[4], (N_EXPERTS, DIM, MOE_HID), dtype=jnp.float32) * s
        Ws_gate = jax.random.normal(ks[5], (SHARED_HID, DIM), dtype=jnp.float32) * s
        Ws_up = jax.random.normal(ks[6], (SHARED_HID, DIM), dtype=jnp.float32) * s
        Ws_down = jax.random.normal(ks[7], (DIM, SHARED_HID), dtype=jnp.float32) * s
        Wsg = jax.random.normal(ks[8], (1, DIM), dtype=jnp.float32) * s
        return {'x': x, 'Wg': Wg, 'We_gate': We_gate, 'We_up': We_up, 'We_down': We_down, 'Ws_gate': Ws_gate, 'Ws_up': Ws_up, 'Ws_down': Ws_down, 'Wsg': Wsg}
    _L1_ffn_all = _L1_ffn_setup()
    _L1_ffn_in = {k: v for k, v in _L1_ffn_all.items() if k in ('Wg', 'We_gate', 'We_up', 'We_down', 'Ws_gate', 'Ws_up', 'Ws_down', 'Wsg')}
    del _L1_ffn_all

    def _L2_xcond_setup():
        import jax, jax.numpy as jnp
        import numpy as np
        B, S, D, H = (2, 256, 128, 16)
        DK = D // H

        def _split_heads(x):
            b, s, _ = x.shape
            return x.reshape(b, s, H, DK).transpose(0, 2, 1, 3)
        key = jax.random.key(seed)
        ks = jax.random.split(key, 14)
        inp = {'query': jax.random.normal(ks[0], (B, S, D), jnp.float32), 'key': jax.random.normal(ks[1], (B, S, D), jnp.float32), 'value': jax.random.normal(ks[2], (B, S, D), jnp.float32), 'tau': jax.random.uniform(ks[3], (B, 1), jnp.float32, 0.5, 1.5), 'delta': jax.random.normal(ks[4], (B, S), jnp.float32)}
        sc = 1.0 / np.sqrt(D)
        for i, name in enumerate(['q', 'k', 'v', 'o']):
            inp[f'W{name}'] = jax.random.normal(ks[5 + 2 * i], (D, D), jnp.float32) * sc
            inp[f'b{name}'] = jax.random.normal(ks[6 + 2 * i], (D,), jnp.float32) * 0.01
        return inp
    _L2_xcond_all = _L2_xcond_setup()
    _L2_xcond_in = {k: v for k, v in _L2_xcond_all.items() if k in ('Wq', 'bq', 'Wk', 'bk', 'Wv', 'bv', 'Wo', 'bo')}
    del _L2_xcond_all

    def _L2_ffn_setup():
        import jax, jax.numpy as jnp
        import numpy as np
        K = 2
        key = jax.random.key(seed)
        ks = jax.random.split(key, 7)
        B, S, D, E = (2, 256, 128, 8)
        H = 4 * D
        sd = 1.0 / np.sqrt(D)
        sh = 1.0 / np.sqrt(H)
        return {'x': jax.random.normal(ks[0], (B, S, D), jnp.float32), 'Wr': jax.random.normal(ks[1], (D, E), jnp.float32) * sd, 'br': jax.random.normal(ks[2], (E,), jnp.float32) * sd, 'W1': jax.random.normal(ks[3], (E, D, H), jnp.float32) * sd, 'b1': jax.random.normal(ks[4], (E, H), jnp.float32) * sd, 'W2': jax.random.normal(ks[5], (E, H, D), jnp.float32) * sh, 'b2': jax.random.normal(ks[6], (E, D), jnp.float32) * sh}
    _L2_ffn_all = _L2_ffn_setup()
    _L2_ffn_in = {k: v for k, v in _L2_ffn_all.items() if k in ('Wr', 'br', 'W1', 'b1', 'W2', 'b2')}
    del _L2_ffn_all

    def _L3_xcond_setup():
        import jax, jax.numpy as jnp
        import numpy as np
        D_MODEL = 128
        N_HEADS = 16
        key = jax.random.key(seed)
        ks = jax.random.split(key, 16)
        B, L, S, D = (4, 256, 256, D_MODEL)
        inp = {'q': jax.random.normal(ks[0], (B, L, D), jnp.float32), 'k': jax.random.normal(ks[1], (B, S, D), jnp.float32), 'v': jax.random.normal(ks[2], (B, S, D), jnp.float32), 'tau': jax.random.uniform(ks[3], (B, 1), jnp.float32, 0.5, 1.5), 'delta': jax.random.normal(ks[4], (B, S), jnp.float32)}
        s = 1.0 / np.sqrt(D)
        inp['Wq'] = jax.random.normal(ks[5], (D, D), jnp.float32) * s
        inp['bq'] = jnp.zeros((D,), jnp.float32)
        inp['Wk'] = jax.random.normal(ks[6], (D, D), jnp.float32) * s
        inp['bk'] = jnp.zeros((D,), jnp.float32)
        inp['Wv'] = jax.random.normal(ks[7], (D, D), jnp.float32) * s
        inp['bv'] = jnp.zeros((D,), jnp.float32)
        inp['Wo'] = jax.random.normal(ks[8], (D, D), jnp.float32) * s
        inp['bo'] = jnp.zeros((D,), jnp.float32)
        return inp
    _L3_xcond_all = _L3_xcond_setup()
    _L3_xcond_in = {k: v for k, v in _L3_xcond_all.items() if k in ('Wq', 'bq', 'Wk', 'bk', 'Wv', 'bv', 'Wo', 'bo')}
    del _L3_xcond_all

    def _L3_ffn_setup():
        import jax, jax.numpy as jnp
        import numpy as np
        N_EXPERTS = 8
        TOP_K = 2
        key = jax.random.key(seed)
        k1, k2, k3, k4 = jax.random.split(key, 4)
        B, T, C, H, E = (2, 256, 128, 512, N_EXPERTS)
        x = jax.random.normal(k1, (B, T, C), dtype=jnp.float32)
        router_w = jax.random.normal(k2, (E, C), dtype=jnp.float32) * 0.02
        w1 = jax.random.normal(k3, (E, C, H), dtype=jnp.float32) * (1.0 / np.sqrt(C))
        w2 = jax.random.normal(k4, (E, H, C), dtype=jnp.float32) * (1.0 / np.sqrt(H))
        return {'x': x, 'router_w': router_w, 'w1': w1, 'w2': w2}
    _L3_ffn_all = _L3_ffn_setup()
    _L3_ffn_in = {k: v for k, v in _L3_ffn_all.items() if k in ('router_w', 'w1', 'w2')}
    del _L3_ffn_all
    return {'x': x, 'ctx_1024': ctx_1024, 'condB_pt': condB_pt, 'condB_tau': condB_tau, 'fside_BxS2_0': fside_BxS2_0, '_lenS2': _lenS2, 'L0_xcond_W_a': _L0_xcond_in['W_a'], 'L0_xcond_W_c': _L0_xcond_in['W_c'], 'L0_ffn_Wg': _L0_ffn_in['Wg'], 'L0_ffn_bg': _L0_ffn_in['bg'], 'L0_ffn_W1': _L0_ffn_in['W1'], 'L0_ffn_b1': _L0_ffn_in['b1'], 'L0_ffn_W2': _L0_ffn_in['W2'], 'L0_ffn_b2': _L0_ffn_in['b2'], 'L0_ffn_gamma': _L0_ffn_in['gamma'], 'L0_ffn_beta': _L0_ffn_in['beta'], 'L1_xcond_Wq': _L1_xcond_in['Wq'], 'L1_xcond_bq': _L1_xcond_in['bq'], 'L1_xcond_Wk': _L1_xcond_in['Wk'], 'L1_xcond_bk': _L1_xcond_in['bk'], 'L1_xcond_Wv': _L1_xcond_in['Wv'], 'L1_xcond_bv': _L1_xcond_in['bv'], 'L1_xcond_Wo': _L1_xcond_in['Wo'], 'L1_xcond_bo': _L1_xcond_in['bo'], 'L1_ffn_Wg': _L1_ffn_in['Wg'], 'L1_ffn_We_gate': _L1_ffn_in['We_gate'], 'L1_ffn_We_up': _L1_ffn_in['We_up'], 'L1_ffn_We_down': _L1_ffn_in['We_down'], 'L1_ffn_Ws_gate': _L1_ffn_in['Ws_gate'], 'L1_ffn_Ws_up': _L1_ffn_in['Ws_up'], 'L1_ffn_Ws_down': _L1_ffn_in['Ws_down'], 'L1_ffn_Wsg': _L1_ffn_in['Wsg'], 'L2_xcond_Wq': _L2_xcond_in['Wq'], 'L2_xcond_bq': _L2_xcond_in['bq'], 'L2_xcond_Wk': _L2_xcond_in['Wk'], 'L2_xcond_bk': _L2_xcond_in['bk'], 'L2_xcond_Wv': _L2_xcond_in['Wv'], 'L2_xcond_bv': _L2_xcond_in['bv'], 'L2_xcond_Wo': _L2_xcond_in['Wo'], 'L2_xcond_bo': _L2_xcond_in['bo'], 'L2_ffn_Wr': _L2_ffn_in['Wr'], 'L2_ffn_br': _L2_ffn_in['br'], 'L2_ffn_W1': _L2_ffn_in['W1'], 'L2_ffn_b1': _L2_ffn_in['b1'], 'L2_ffn_W2': _L2_ffn_in['W2'], 'L2_ffn_b2': _L2_ffn_in['b2'], 'L3_xcond_Wq': _L3_xcond_in['Wq'], 'L3_xcond_bq': _L3_xcond_in['bq'], 'L3_xcond_Wk': _L3_xcond_in['Wk'], 'L3_xcond_bk': _L3_xcond_in['bk'], 'L3_xcond_Wv': _L3_xcond_in['Wv'], 'L3_xcond_bv': _L3_xcond_in['bv'], 'L3_xcond_Wo': _L3_xcond_in['Wo'], 'L3_xcond_bo': _L3_xcond_in['bo'], 'L3_ffn_router_w': _L3_ffn_in['router_w'], 'L3_ffn_w1': _L3_ffn_in['w1'], 'L3_ffn_w2': _L3_ffn_in['w2']}

def reference(x, ctx_1024, condB_pt, condB_tau, fside_BxS2_0, _lenS2, L0_xcond_W_a, L0_xcond_W_c, L0_ffn_Wg, L0_ffn_bg, L0_ffn_W1, L0_ffn_b1, L0_ffn_W2, L0_ffn_b2, L0_ffn_gamma, L0_ffn_beta, L1_xcond_Wq, L1_xcond_bq, L1_xcond_Wk, L1_xcond_bk, L1_xcond_Wv, L1_xcond_bv, L1_xcond_Wo, L1_xcond_bo, L1_ffn_Wg, L1_ffn_We_gate, L1_ffn_We_up, L1_ffn_We_down, L1_ffn_Ws_gate, L1_ffn_Ws_up, L1_ffn_Ws_down, L1_ffn_Wsg, L2_xcond_Wq, L2_xcond_bq, L2_xcond_Wk, L2_xcond_bk, L2_xcond_Wv, L2_xcond_bv, L2_xcond_Wo, L2_xcond_bo, L2_ffn_Wr, L2_ffn_br, L2_ffn_W1, L2_ffn_b1, L2_ffn_W2, L2_ffn_b2, L3_xcond_Wq, L3_xcond_bq, L3_xcond_Wk, L3_xcond_bk, L3_xcond_Wv, L3_xcond_bv, L3_xcond_Wo, L3_xcond_bo, L3_ffn_router_w, L3_ffn_w1, L3_ffn_w2):
    import jax
    import jax.numpy as jnp

    def _L0_xcond_ref(encoder_outputs, decoder_h_t, src_len, p_t, W_a, W_c):
        import jax, jax.numpy as jnp
        import numpy as np
        N, L, H, Q = (64, 258, 128, 32)
        WINDOW = 16.0
        DEV_POW = 128.0
        n, l, h = encoder_outputs.shape
        idx = jnp.arange(l, dtype=jnp.float32)
        src_end = src_len.astype(jnp.float32)
        attn_start = jnp.maximum(p_t - WINDOW, 0.0)
        attn_end = jnp.minimum(p_t + WINDOW, src_end)
        mask = (idx[None, :] < attn_start[:, None]) | (idx[None, :] > attn_end[:, None])
        score = jnp.einsum('nqh,hk,nlk->nql', decoder_h_t, W_a, encoder_outputs)
        score = jnp.where(mask[:, None, :], -1000000000.0, score)
        align = jax.nn.softmax(score, axis=2)
        gauss = jnp.exp(-(idx[None, :] - p_t[:, None]) ** 2 / DEV_POW)
        align = align * gauss[:, None, :]
        context = jnp.einsum('nql,nlh->nqh', align, encoder_outputs)
        cat = jnp.concatenate([context, decoder_h_t], axis=2)
        return jnp.tanh(cat @ W_c.T)

    def _L0_ffn_ref(x, Wg, bg, W1, b1, W2, b2, gamma, beta):
        import jax, jax.numpy as jnp
        import numpy as np
        D = 128
        H = 512
        E = 8
        B = 2
        T = 256
        LN_EPS = 1e-05

        def _layer_norm(r, gamma, beta):
            mu = jnp.mean(r, axis=-1, keepdims=True)
            var = jnp.mean(jnp.square(r - mu), axis=-1, keepdims=True)
            return (r - mu) * jax.lax.rsqrt(var + LN_EPS) * gamma + beta
        logits = jnp.einsum('btd,de->bte', x, Wg) + bg
        top2_vals, top2_idx = jax.lax.top_k(logits, 2)
        scores = jax.nn.softmax(top2_vals, axis=-1)
        onehot = jax.nn.one_hot(top2_idx, E, dtype=x.dtype)
        combine = jnp.einsum('btk,btke->bte', scores, onehot)
        h = jnp.einsum('btd,edh->bteh', x, W1) + b1[None, None]
        h = jax.nn.gelu(h, approximate=False)
        y = jnp.einsum('bteh,ehd->bted', h, W2) + b2[None, None]
        out = jnp.einsum('bted,bte->btd', y, combine)
        return _layer_norm(x + out, gamma, beta)

    def _L1_xcond_ref(q, k, v, tau, delta, Wq, bq, Wk, bk, Wv, bv, Wo, bo):
        import jax, jax.numpy as jnp
        import numpy as np
        D_MODEL = 128
        N_HEADS = 16
        B, L, D = q.shape
        S = k.shape[1]
        H = N_HEADS
        E = D // H
        qh = (q @ Wq.T + bq).reshape(B, L, H, E)
        kh = (k @ Wk.T + bk).reshape(B, S, H, E)
        vh = (v @ Wv.T + bv).reshape(B, S, H, E)
        scale = 1.0 / np.sqrt(E).astype(np.float32)
        scores = jnp.einsum('blhe,bshe->bhls', qh, kh)
        scores = scores * tau[:, None, None, :] + delta[:, None, None, :]
        a = jax.nn.softmax(scale * scores, axis=-1)
        out = jnp.einsum('bhls,bshd->blhd', a, vh).reshape(B, L, D)
        return out @ Wo.T + bo

    def _L1_ffn_ref(x, Wg, We_gate, We_up, We_down, Ws_gate, Ws_up, Ws_down, Wsg):
        import jax, jax.numpy as jnp
        import numpy as np
        DIM = 128
        MOE_HID = 64
        SHARED_HID = 256
        N_EXPERTS = 16
        TOP_K = 2
        NORM_TOPK_PROB = True
        B, S, D = x.shape
        xt = x.reshape(-1, D)
        gates = jax.nn.softmax(xt @ Wg.T, axis=-1)
        scores, inds = jax.lax.top_k(gates, TOP_K)
        if NORM_TOPK_PROB:
            scores = scores / jnp.sum(scores, axis=-1, keepdims=True)
        g = jnp.einsum('td,ehd->teh', xt, We_gate)
        u = jnp.einsum('td,ehd->teh', xt, We_up)
        h = jax.nn.silu(g) * u
        y_all = jnp.einsum('teh,edh->ted', h, We_down)
        y_sel = jnp.take_along_axis(y_all, inds[:, :, None], axis=1)
        y = jnp.sum(y_sel * scores[:, :, None], axis=1)
        shared = jax.nn.silu(xt @ Ws_gate.T) * (xt @ Ws_up.T) @ Ws_down.T
        y = y + jax.nn.sigmoid(xt @ Wsg.T) * shared
        return y.reshape(B, S, D)

    def _L2_xcond_ref(query, key, value, tau, delta, Wq, bq, Wk, bk, Wv, bv, Wo, bo):
        import jax, jax.numpy as jnp
        import numpy as np
        B, S, D, H = (2, 256, 128, 16)
        DK = D // H

        def _split_heads(x):
            b, s, _ = x.shape
            return x.reshape(b, s, H, DK).transpose(0, 2, 1, 3)
        q = _split_heads(query @ Wq.T + bq)
        k = _split_heads(key @ Wk.T + bk)
        v = _split_heads(value @ Wv.T + bv)
        scores = jnp.einsum('bhqd,bhkd->bhqk', q, k)
        scores = scores * tau[:, :, None, None] + delta[:, None, None, :]
        scores = scores / jnp.sqrt(jnp.asarray(DK, scores.dtype))
        p_attn = jax.nn.softmax(scores, axis=-1)
        x = jnp.einsum('bhqk,bhkd->bhqd', p_attn, v)
        x = x.transpose(0, 2, 1, 3).reshape(query.shape[0], -1, H * DK)
        return x @ Wo.T + bo

    def _L2_ffn_ref(x, Wr, br, W1, b1, W2, b2):
        import jax, jax.numpy as jnp
        import numpy as np
        K = 2
        E = Wr.shape[-1]
        scores = jnp.einsum('bsd,de->bse', x, Wr) + br
        _, topk_idx = jax.lax.top_k(scores, K)
        indicator = jax.nn.one_hot(topk_idx, E, dtype=scores.dtype).sum(-2)
        neg_inf = jnp.asarray(-jnp.inf, scores.dtype)
        weights = jax.nn.softmax(jnp.where(indicator > 0, scores, neg_inf), axis=-1)
        out = jnp.zeros_like(x)
        for i in range(E):
            xi = x * indicator[..., i:i + 1]
            h = jax.nn.relu(jnp.einsum('bsd,dh->bsh', xi, W1[i]) + b1[i])
            yi = jnp.einsum('bsh,hd->bsd', h, W2[i]) + b2[i]
            out = out + yi * weights[..., i:i + 1]
        return out

    def _L3_xcond_ref(q, k, v, tau, delta, Wq, bq, Wk, bk, Wv, bv, Wo, bo):
        import jax, jax.numpy as jnp
        import numpy as np
        D_MODEL = 128
        N_HEADS = 16
        B, L, D = q.shape
        S = k.shape[1]
        H = N_HEADS
        E = D // H
        qh = (q @ Wq.T + bq).reshape(B, L, H, E)
        kh = (k @ Wk.T + bk).reshape(B, S, H, E)
        vh = (v @ Wv.T + bv).reshape(B, S, H, E)
        scale = 1.0 / np.sqrt(E).astype(np.float32)
        scores = jnp.einsum('blhe,bshe->bhls', qh, kh)
        scores = scores * tau[:, None, None, :] + delta[:, None, None, :]
        a = jax.nn.softmax(scale * scores, axis=-1)
        out = jnp.einsum('bhls,bshd->blhd', a, vh).reshape(B, L, D)
        return out @ Wo.T + bo

    def _L3_ffn_ref(x, router_w, w1, w2):
        import jax, jax.numpy as jnp
        import numpy as np
        N_EXPERTS = 8
        TOP_K = 2
        B, T, C = x.shape
        E = N_EXPERTS
        xf = x.reshape(-1, C)
        logits = jnp.einsum('nc,ec->ne', xf, router_w)
        probs = jax.nn.softmax(logits, axis=-1)
        top_w, top_i = jax.lax.top_k(probs, TOP_K)
        top_w = top_w / jnp.sum(top_w, axis=-1, keepdims=True)
        comb = jnp.einsum('nk,nke->ne', top_w, jax.nn.one_hot(top_i, E, dtype=xf.dtype))
        h = jax.nn.gelu(jnp.einsum('nc,ech->enh', xf, w1), approximate=False)
        y = jnp.einsum('enh,ehc->enc', h, w2)
        out = jnp.einsum('ne,enc->nc', comb, y)
        return out.reshape(B, T, C)
    x = x + _L0_xcond_ref(ctx_1024, _layernorm(x, axis=-1), _lenS2, condB_pt, L0_xcond_W_a, L0_xcond_W_c)
    x = x + _L0_ffn_ref(_layernorm(x, axis=-1), L0_ffn_Wg, L0_ffn_bg, L0_ffn_W1, L0_ffn_b1, L0_ffn_W2, L0_ffn_b2, L0_ffn_gamma, L0_ffn_beta)
    x = x + _L1_xcond_ref(_layernorm(x, axis=-1), ctx_1024, ctx_1024, condB_tau[:, None], fside_BxS2_0, L1_xcond_Wq, L1_xcond_bq, L1_xcond_Wk, L1_xcond_bk, L1_xcond_Wv, L1_xcond_bv, L1_xcond_Wo, L1_xcond_bo)
    x = x + _L1_ffn_ref(_layernorm(x, axis=-1), L1_ffn_Wg, L1_ffn_We_gate, L1_ffn_We_up, L1_ffn_We_down, L1_ffn_Ws_gate, L1_ffn_Ws_up, L1_ffn_Ws_down, L1_ffn_Wsg)
    x = x + _L2_xcond_ref(_layernorm(x, axis=-1), ctx_1024, ctx_1024, condB_tau[:, None], fside_BxS2_0, L2_xcond_Wq, L2_xcond_bq, L2_xcond_Wk, L2_xcond_bk, L2_xcond_Wv, L2_xcond_bv, L2_xcond_Wo, L2_xcond_bo)
    x = x + _L2_ffn_ref(_layernorm(x, axis=-1), L2_ffn_Wr, L2_ffn_br, L2_ffn_W1, L2_ffn_b1, L2_ffn_W2, L2_ffn_b2)
    x = x + _L3_xcond_ref(_layernorm(x, axis=-1), ctx_1024, ctx_1024, condB_tau[:, None], fside_BxS2_0, L3_xcond_Wq, L3_xcond_bq, L3_xcond_Wk, L3_xcond_bk, L3_xcond_Wv, L3_xcond_bv, L3_xcond_Wo, L3_xcond_bo)
    x = x + _L3_ffn_ref(_layernorm(x, axis=-1), L3_ffn_router_w, L3_ffn_w1, L3_ffn_w2)
    return x

_drawn_inputs = setup_inputs


def setup_inputs(seed=0):
    import zlib

    import numpy as np

    out = dict(_drawn_inputs(seed))
    spreads = {'L0_ffn_gamma': (1.0, 0.2),
     'L0_ffn_beta': (0.0, 0.1),
     'L1_xcond_bq': (0.0, 0.38),
     'L1_xcond_bk': (0.0, 2.0),
     'L1_xcond_bv': (0.0, 0.1),
     'L1_xcond_bo': (0.0, 0.1),
     'L3_xcond_bq': (0.0, 0.537),
     'L3_xcond_bk': (0.0, 2.0),
     'L3_xcond_bv': (0.0, 0.1),
     'L3_xcond_bo': (0.0, 0.1)}
    factors = {'L0_ffn_b1': 3.095,
     'L1_ffn_Wg': 6.564,
     'L1_ffn_We_gate': 5.496,
     'L1_ffn_We_up': 6.187,
     'L1_ffn_We_down': 5.51,
     'L1_ffn_Ws_gate': 5.391,
     'L1_ffn_Ws_up': 5.394,
     'L1_ffn_Ws_down': 5.256,
     'L1_ffn_Wsg': 8.0,
     'L2_xcond_bq': 34.853,
     'L2_xcond_bk': 64.0,
     'L2_xcond_bv': 3.605,
     'L2_xcond_bo': 3.987,
     'L2_ffn_b2': 2.758}
    for name, (base, spread) in spreads.items():
        noise = np.random.default_rng([zlib.crc32(name.encode()), seed]).standard_normal(out[name].shape)
        drawn = base * np.exp(spread * noise) if base else spread * noise
        out[name] = jnp.asarray(drawn.astype(out[name].dtype))
    for name, factor in factors.items():
        out[name] = (out[name] * factor).astype(out[name].dtype)
    return out
```

```python
from contextlib import ExitStack

import concourse.bass as bass
from concourse import mybir

F32 = mybir.dt.float32
I32 = mybir.dt.int32
U32 = mybir.dt.uint32
ALU = mybir.AluOpType
ACT = mybir.ActivationFunctionType
AX_X = mybir.AxisListType.X

P = 128
NB = 16
GB = 4
NG = NB // GB
GT = GB * P
KEYS = 120
GK = GB * KEYS
H, HD = 16, 8
ROW = 32
NJ = 4
M_ROW = 24
D_ROW = 28
E8, HID, HC = 8, 512, 4
E16, CH1 = 16, 10
LN_EPS = 1e-5
WINDOW, DEV_POW = 16.0, 128.0
MASKED = 1.0e9
SCALE = float(HD) ** -0.5

LINKS = {"x0": 11, "x": 7, "f0": 12, "f1": 18, "f2": 7, "f3": 7}


LN_OF = [0, NG, 3 * NG, 4 * NG, 5 * NG, 6 * NG, 7 * NG, 8 * NG]
LN_TOTAL = 9 * NG
MOE_F = [0, 2, 3]
MOE_FRONT = [1, 5, 7]


def pair_rows(w):
    return w.rearrange("e h d -> (e h) d").rearrange("(c a) d -> a c d", a=P)


def build(nc, t, out):
    ctx = ExitStack()
    with ctx:
        def sb(name, shape, dt=F32):
            return ctx.enter_context(nc.sbuf_tensor(name, shape, dt))

        def sem(name):
            return ctx.enter_context(nc.semaphore(name))

        x = sb("x", [P, NB * P])
        xn = sb("xn", [P, GT])
        xnT = sb("xnT", [P, GT])
        ctxT = sb("ctxT", [P, NB * KEYS])
        ctx_g = sb("ctx_g", [KEYS, GB, P])
        ctxT_g = sb("ctxT_g", [P, GK])
        ident = sb("ident", [P, P])
        wq = [sb(f"wq{i}", [P, H * ROW]) for i in range(3)]
        wk = [sb(f"wk{i}", [P, H * ROW]) for i in range(3)]
        wvT = [sb(f"wvT{i}", [P, P]) for i in range(3)]
        woT = [sb(f"woT{i}", [P, P]) for i in range(3)]
        bv = [sb(f"bv{i}", [P, P]) for i in range(3)]
        bo = [sb(f"bo{i}", [P, P]) for i in range(3)]
        bqs = [sb(f"bqs{i}", [P, NJ]) for i in range(3)]
        bks = [sb(f"bks{i}", [P, NJ]) for i in range(3)]
        q_bias = [sb(f"q_bias{i}", [P, NJ, NB]) for i in range(3)]
        k_bias = [sb(f"k_bias{i}", [P, NJ]) for i in range(3)]
        special = sb("special", [P, NJ + 1])
        deltaK = sb("deltaK", [P, NB * KEYS])
        waT = sb("waT", [P, P])
        wcT = sb("wcT", [P, 2, P])
        moeA = sb("moeA", [P, 2 * E8 * HID])
        moeB = sb("moeB", [P, 2 * E8 * HID])
        nat = moeB[:, :].rearrange("p (s c) -> p s c", c=P)
        geT = sb("geT", [P, CH1 * P])
        upT = sb("upT", [P, CH1 * P])
        dnT = sb("dnT", [P, CH1, P])
        r0 = sb("r0", [P, E8])
        r1 = sb("r1", [P, E16 + 1])
        r2 = sb("r2", [P, E8])
        r3 = sb("r3", [P, E8])
        rb0 = sb("rb0", [P, E8])
        rb2 = sb("rb2", [P, E8])
        b1T = sb("b1T", [P, 2 * E8 * HC])
        b2_0 = sb("b2_0", [E8, P])
        b2_2 = sb("b2_2", [E8, P])
        gamma = sb("gamma", [P, P])
        beta = sb("beta", [P, P])
        tau = sb("tau", [P, NB])
        pt = sb("pt", [P, NB])
        lens_i = sb("lens_i", [P, NB], I32)
        lens = sb("lens", [P, NB])
        w_lo = sb("w_lo", [P, NB])
        w_hi = sb("w_hi", [P, NB])
        iota_i = sb("iota_i", [P, P], I32)
        iota = sb("iota", [P, P])
        half = sb("half", [P, GB])
        sel = sb("sel", [E16 + 1, CH1 * P])
        stats = sb("stats", [P, GB, 6])
        mv = sb("mv", [P, GB, 2])
        vpe = sb("vpe", [P, GB])
        rstd = sb("rstd", [P, GB])
        rstd_t = sb("rstd_t", [P, GB])
        qs = sb("qs", [P, NJ, GT])
        ks = sb("ks", [P, NJ, GK])
        vaug = sb("vaug", [KEYS, GB, H, HD + 1])
        probs = sb("probs", [P, 4 * 512])
        m_pad = sb("m_pad", [P, P])
        rden = sb("rden", [P, GB, H])
        attn = sb("attn", [P, GT])
        attnT = sb("attnT", [P, GT])
        tmp = sb("tmp", [P, GT])
        tmp2 = sb("tmp2", [P, GT])
        lg = sb("lg", [P, GB, E16 + 1])
        mx = sb("mx", [P, GB, 8])
        ix = sb("ix", [P, GB, 8], U32)
        ixf = sb("ixf", [P, GB, 2])
        oh1 = sb("oh1", [P, GB, E16])
        oh2 = sb("oh2", [P, GB, E16])
        gap = sb("gap", [P, GB])
        th = sb("th", [P, GB])
        ths = sb("ths", [P, GB])
        w1 = sb("w1", [P, GB])
        w2 = sb("w2", [P, GB])
        comb = sb("comb", [P, GB, E16 + 1])
        combT = sb("combT", [E16 + 1, GT])
        hT = [sb(f"hT{i}", [P, HC, GT]) for i in range(2)]

        psS = ctx.enter_context(nc.psum_tensor("psS", [P, 4, 512], F32))
        psH = ctx.enter_context(nc.psum_tensor("psH", [P, 2, 512], F32))
        psY = ctx.enter_context(nc.psum_tensor("psY", [P, 512], F32))
        psM = ctx.enter_context(nc.psum_tensor("psM", [P, 512], F32))

        names = """x_in nat_in small_in moeA_in moeB_in ctx_g_in ctxT_g_in out_done
            zeroed consts_ready pool_step prep_ps prep_sb vec_step tables_ready
            ln_var ln_vpe ln_rstd xn_ready xnT_ps xnT_ready
            wa_ps wa_ready score_ps gauss_arg gauss_ready x0_shifted x0_exp_ready align_ready alignT_ps alignT_ready
            context_ps context_ready mix_ps tanh_ready x0_done
            k_ps k_ready v_ps v_ready q_ps q_ready a_ps max_ready maxT_ps q_shifted b_ps probs_ready o_ps attn_ready
            attnT_ps attnT_ready wo_ps x_done
            logits_ps gap_ready gate_ready comb_ready combT_ps combT_ready b2_ps b2_added
            h_ps h_ready y_ps y_added f0_done
            f1_ps silu_ready f1_h_ready f1_down f1_yT_ready f1_y_ps f1_done""".split()
        s = {n: sem(n) for n in names}

        def bc_row(row, n):
            return row.rearrange("(a n) -> a n", a=1).broadcast_to([P, n])

        def tok(buf, b=0, n=1):
            return buf[:, b * P:(b + n) * P]

        def tiles(ap2d, n=GB):
            return ap2d.rearrange("p (b c) -> p b c", b=n)

        def x_tile(g, b):
            return x[:, bass.ds(g * GT + b * P, P)]

        def x_group(g):
            return x[:, bass.ds(g * GT, GT)]

        def w1_of(home):
            return home[:, 0:E8 * HID]

        def w2_of(home):
            return home[:, E8 * HID:].rearrange("p (e k d) -> p e k d", e=E8, k=HC)

        SLOTS = 64
        rows_of = [KEYS] * NB + [P] * (SLOTS - NB)
        rows_of[61], rows_of[62], rows_of[63] = E16 + 1, E8, 2 * E8 * HC
        NAT_DMAS, SMALL_DMAS, MOE_DMAS = 26, 17 + 4 * 7, 1 + E8
        PREPS = SLOTS // 4

        def gate_bank(c):
            return psS[:, 1, :] if c % 2 else psH[:, 0, :]

        def up_bank(c):
            return psS[:, 2, :] if c % 2 else psH[:, 1, :]

        def weight_bank(c):
            return psS[:, 3, :] if c % 2 else psS[:, 0, :]

        block = ctx.enter_context(nc.Block())

        @block.sync
        def _(sp):
            count = [0]

            def nat_load(dst, src):
                count[0] += 1
                sp.dma_start(dst, src).then_inc(s["nat_in"], 16)

            def moe_load(home, w1d, w2d, done):
                sp.dma_start(w1_of(home).rearrange("p (e h) -> p e h", e=E8), w1d.rearrange("e d h -> d e h")).then_inc(done, 16)
                for e in range(E8):
                    sp.dma_start(w2_of(home)[:, e], w2d[e].rearrange("(k p) d -> p k d", k=HC)).then_inc(done, 16)

            nat_load(nat[0:KEYS, 0:NB, :], t["ctx_1024"].rearrange("b k d -> k b d"))
            nat_load(nat[:, 16, :], t["L0_xcond_W_a"])
            nat_load(nat[:, 17:19, :], t["L0_xcond_W_c"].rearrange("o (h k) -> o h k", h=2))
            sp.dma_start(tiles(x[:, :], NB), t["x"].rearrange("b p d -> p b d")).then_inc(s["x_in"], 16)
            for i in range(3):
                for m, w in enumerate("qkvo"):
                    nat_load(nat[:, 19 + 4 * i + m, :], t[f"L{i + 1}_xcond_W{w}"])
            nat_load(nat[:, 31:39, :], pair_rows(t["L1_ffn_We_gate"]))
            nat_load(nat[:, 39:47, :], pair_rows(t["L1_ffn_We_up"]))
            nat_load(nat[:, 47:49, :], t["L1_ffn_Ws_gate"].rearrange("(c h) d -> h c d", c=2))
            nat_load(nat[:, 49:51, :], t["L1_ffn_Ws_up"].rearrange("(c h) d -> h c d", c=2))
            nat_load(nat[:, 51:59, :].rearrange("p c (a h) -> p (c a) h", a=2), t["L1_ffn_We_down"].rearrange("e d h -> d e h"))
            nat_load(nat[:, 59:61, :], t["L1_ffn_Ws_down"].rearrange("d (c h) -> d c h", c=2))
            nat_load(nat[0:E16, 61, :], t["L1_ffn_Wg"])
            nat_load(nat[E16:E16 + 1, 61, :], t["L1_ffn_Wsg"])
            nat_load(nat[0:E8, 62, :], t["L3_ffn_router_w"])
            nat_load(nat[0:32, 63, :], t["L0_ffn_b1"].rearrange("e (k p) -> (e k) p", k=HC))
            nat_load(nat[32:64, 63, :], t["L2_ffn_b1"].rearrange("e (k p) -> (e k) p", k=HC))
            assert count[0] == NAT_DMAS, count
            moe_load(moeA, t["L0_ffn_W1"], t["L0_ffn_W2"], s["moeA_in"])
            sp.dma_start(ctx_g[:, :, :], t["ctx_1024"][0:GB].rearrange("b k d -> k b d")).then_inc(s["ctx_g_in"], 16)
            with sp.Fori(1, NG) as g:
                sp.wait_ge(s["context_ps"], g)
                sp.dma_start(ctx_g[:, :, :], t["ctx_1024"][bass.ds(g * GB, GB)].rearrange("b k d -> k b d")).then_inc(s["ctx_g_in"], 16)
            sp.wait_ge(s["prep_ps"], PREPS)
            moe_load(moeB, t["L2_ffn_W1"], t["L2_ffn_W2"], s["moeB_in"])
            sp.wait_ge(s["prep_sb"], PREPS)
            for i in range(3):
                if i == 0:
                    sp.dma_start(ctxT_g[:, :], ctxT[:, 0:GK]).then_inc(s["ctxT_g_in"], 16)
                with sp.Fori(1 if i == 0 else 0, NG) as g:
                    sp.wait_ge(s["v_ps"], NG * i + g)
                    sp.dma_start(ctxT_g[:, :], ctxT[:, bass.ds(g * GK, GK)]).then_inc(s["ctxT_g_in"], 16)
                if i == 0:
                    sp.wait_ge(s["y_added"], NG * E8)
                    moe_load(moeA, t["L3_ffn_w1"], t["L3_ffn_w2"], s["moeA_in"])
            sp.wait_ge(s["y_added"], 3 * NG * E8)
            sp.dma_start(out.rearrange("b p d -> p b d"), tiles(x[:, :], NB)).then_inc(s["out_done"], 16)
            sp.wait_ge(s["out_done"], 16)

        @block.gpsimd
        def _(pool):
            pool.memset(ident[:], 0.0).then_inc(s["pool_step"], 1)
            pool.memset(sel[:], 0.0).then_inc(s["pool_step"], 1)
            pool.memset(half[:], -0.5).then_inc(s["pool_step"], 1)
            pool.memset(special[:], 0.0).then_inc(s["pool_step"], 1)
            pool.wait_ge(s["pool_step"], 4)
            pool.affine_select(out=ident[:], in_=ident[:], compare_op=ALU.not_equal, fill=1.0, base=0,
                               pattern=[[-1, P]], channel_multiplier=1).then_inc(s["consts_ready"], 1)
            for r in range(4):
                pool.affine_select(out=special[:], in_=special[:], compare_op=ALU.not_equal, fill=-1.0,
                                   base=-ROW * r - M_ROW, pattern=[[-1, NJ + 1]], channel_multiplier=1).then_inc(s["pool_step"], 1)
                pool.wait_ge(s["pool_step"], 5 + r)
            halves = sel[:, :].rearrange("e (q p) -> e q p", p=P // 2)
            pool.affine_select(out=halves[:, 0:E16, :], in_=halves[:, 0:E16, :], compare_op=ALU.not_equal, fill=1.0,
                               base=0, pattern=[[-1, E16], [0, P // 2]], channel_multiplier=1).then_inc(s["consts_ready"], 1)
            pool.affine_select(out=halves[:, E16:, :], in_=halves[:, E16:, :], compare_op=ALU.not_equal, fill=1.0,
                               base=-E16, pattern=[[0, 2 * CH1 - E16], [0, P // 2]], channel_multiplier=1).then_inc(s["consts_ready"], 1)
            pool.iota(iota_i[:, :], [[1, P]], base=0, channel_multiplier=0).then_inc(s["consts_ready"], 1)

            with pool.Fori(0, LN_TOTAL) as n:
                norm = pool.to_reg(n + 1)
                pool.wait_ge(s["consts_ready"], 4)
                pool.wait_ge(s["ln_var"], norm)
                pool.tensor_scalar(vpe[:], mv[:, :, 1], LN_EPS, None, ALU.add).then_inc(s["ln_vpe"], 1)
                pool.wait_ge(s["ln_vpe"], n + 1)
                pool.tensor_tensor(rstd[:], vpe[:], half[:], ALU.pow).then_inc(s["ln_rstd"], 1)

        @block.scalar
        def _(act):
            count = [0]

            def small(dst, src, **kw):
                count[0] += 1
                act.dma_start(dst, src, **kw).then_inc(s["small_in"], 16)

            small(tau[:, :], bc_row(t["condB_tau"], NB))
            small(pt[:, :], bc_row(t["condB_pt"], NB))
            small(lens_i[:, :], bc_row(t["_lenS2"], NB))
            small(r0[:, :], t["L0_ffn_Wg"])
            small(rb0[:, :], bc_row(t["L0_ffn_bg"], E8))
            small(r2[:, :], t["L2_ffn_Wr"])
            small(rb2[:, :], bc_row(t["L2_ffn_br"], E8))
            small(b2_0[:, :], t["L0_ffn_b2"])
            small(b2_2[:, :], t["L2_ffn_b2"])
            small(gamma[:, :], bc_row(t["L0_ffn_gamma"], P))
            small(beta[:, :], bc_row(t["L0_ffn_beta"], P))
            for i in range(3):
                small(bv[i][:, :], bc_row(t[f"L{i + 1}_xcond_bv"], P))
                small(bo[i][:, :], bc_row(t[f"L{i + 1}_xcond_bo"], P))
            act.wait_ge(s["zeroed"], 1)
            for r in range(4):
                for i in range(3):
                    for dst, nm in ((bqs, "bq"), (bks, "bk")):
                        small(dst[i][ROW * r:ROW * r + HD, :],
                              t[f"L{i + 1}_xcond_{nm}"].rearrange("(j r d) -> r d j", j=NJ, r=4)[r], allow_slow_non_contiguous=True)
                small(deltaK[ROW * r + D_ROW:ROW * r + D_ROW + 1, :], t["fside_BxS2_0"].rearrange("(a b) k -> a (b k)", a=1))
            assert count[0] == SMALL_DMAS, count

            def copy_out(dst, src, done):
                act.activation(dst, src, ACT.Copy).then_inc(s[done], 1)

            def front(n):
                act.wait_ge(s["xnT_ps"], n + 1)
                copy_out(xnT[:, :], psM[:, :], "xnT_ready")

            def window_attention(g):
                act.wait_ge(s["wa_ps"], g + 1)
                copy_out(attn[:, 0:GK], psH[:, 0, 0:GK], "wa_ready")
                act.wait_ge(s["gauss_arg"], g + 1)
                act.activation(tmp2[:, 0:GK], tmp2[:, 0:GK], ACT.Exp, scale=-1.0 / DEV_POW).then_inc(s["gauss_ready"], 1)
                front(g)
                act.wait_ge(s["x0_shifted"], g + 1)
                act.activation(probs[:, 0:GK], probs[:, 0:GK], ACT.Exp).then_inc(s["x0_exp_ready"], 1)
                act.wait_ge(s["alignT_ps"], g + 1)
                copy_out(probs[0:KEYS, 1024:1024 + GT], psM[0:KEYS, :], "alignT_ready")
                act.wait_ge(s["context_ps"], g + 1)
                copy_out(attnT[:, :], psY[:, :], "context_ready")
                act.wait_ge(s["mix_ps"], g + 1)
                act.activation(tmp[:, :], psH[:, 1, :], ACT.Tanh).then_inc(s["tanh_ready"], 1)

            def moe(li, g, func, b1):
                f, m = MOE_F[li] * NG + g, li * NG + g
                front(MOE_FRONT[li] * NG + g)
                act.wait_ge(s["gap_ready"], f + 1)
                act.activation(th[:], gap[:], ACT.Tanh, scale=0.5).then_inc(s["gate_ready"], 1)
                act.wait_ge(s["combT_ps"], f + 1)
                copy_out(combT[0:E8, :], psM[0:E8, :], "combT_ready")
                for c in range(E8 * HC):
                    e, k = divmod(c, HC)
                    act.wait_ge(s["h_ps"], m * (E8 * HC) + c + 1)
                    if e >= 2:
                        act.wait_ge(s["y_ps"], m * E8 + e - 1)
                    if b1 is None:
                        act.activation(hT[e % 2][:, k, :], psH[:, c % 2, :], func).then_inc(s["h_ready"], 1)
                    else:
                        act.activation(hT[e % 2][:, k, :], psH[:, c % 2, :], func,
                                       bias=b1T[:, b1 + c:b1 + c + 1]).then_inc(s["h_ready"], 1)

            def attention(i, g):
                a = i * NG + g
                front((2 * i + 2) * NG + g)
                for b in range(GB):
                    act.wait_ge(s["b_ps"], a * GB + b + 1)
                    if b:
                        act.wait_ge(s["o_ps"], a * GB + b)
                    act.activation(probs[0:KEYS, :], psS[0:KEYS, :, :].rearrange("p r c -> p (r c)"), ACT.Exp,
                                   scale=SCALE).then_inc(s["probs_ready"], 1)
                act.wait_ge(s["attnT_ps"], a + 1)
                copy_out(attnT[:, :], psH[:, 1, :], "attnT_ready")

            def gated(g):
                f = NG + g
                front(3 * NG + g)
                act.wait_ge(s["gap_ready"], f + 1)
                act.activation(th[:], gap[:], ACT.Tanh, scale=0.5)
                act.activation(ths[:], lg[:, :, E16], ACT.Tanh, scale=0.5).then_inc(s["gate_ready"], 1)
                act.wait_ge(s["combT_ps"], f + 1)
                copy_out(combT[:, :], psM[0:E16 + 1, :], "combT_ready")
                for c in range(CH1):
                    act.wait_ge(s["f1_ps"], g * CH1 + c + 1)
                    if c >= 2:
                        act.wait_ge(s["f1_h_ready"], g * CH1 + c - 1)
                    act.activation(hT[c % 2][:, 0, :], gate_bank(c), ACT.Silu).then_inc(s["silu_ready"], 1)
                act.wait_ge(s["f1_down"], g * CH1 + CH1)
                copy_out(attnT[:, :], psY[:, :], "f1_yT_ready")

            with act.Fori(0, NG) as g:
                window_attention(g)
            with act.Fori(0, NG) as g:
                moe(0, g, ACT.Gelu, 0)
            with act.Fori(0, NG) as g:
                attention(0, g)
            with act.Fori(0, NG) as g:
                gated(g)
            with act.Fori(0, NG) as g:
                attention(1, g)
            with act.Fori(0, NG) as g:
                moe(1, g, ACT.Relu, E8 * HC)
            with act.Fori(0, NG) as g:
                attention(2, g)
            with act.Fori(0, NG) as g:
                moe(2, g, ACT.Gelu, None)

        @block.vector
        def _(dve):
            chain = {"n": 0, "base": 0, "per": 0, "g": 0}

            def link(ins, alone=False):
                chain["n"] += 1
                ins.then_inc(s["vec_step"], 1)
                value = chain["g"] * chain["per"] + (chain["base"] + chain["n"])
                if alone:
                    value = dve.to_reg(value)
                    dve.wait_ge(s["consts_ready"], 4)
                dve.wait_ge(s["vec_step"], value)

            def stage(kind, body):
                chain["base"] += chain["n"]
                chain["per"] = LINKS[kind]
                with dve.Fori(0, NG) as g:
                    chain["n"], chain["g"] = 0, g
                    body(g)
                    assert chain["n"] == LINKS[kind], (kind, chain["n"])
                chain["base"] += NG * LINKS[kind]
                chain["n"], chain["g"] = 0, 0

            def memset(buf, v):
                return dve.memset(buf, v)

            for i in range(3):
                memset(bqs[i][:, :], 0.0)
                memset(bks[i][:, :], 0.0)
                memset(wq[i][:, :], 0.0)
                memset(wk[i][:, :], 0.0)
            memset(deltaK[:, :], 0.0).then_inc(s["zeroed"], 1)
            memset(vaug[:, :, :, :], 1.0)
            link(memset(m_pad[:, :], 0.0))
            dve.wait_ge(s["consts_ready"], 4)
            link(dve.tensor_copy(iota[:, :], iota_i[:, :]))
            dve.wait_ge(s["small_in"], 16 * SMALL_DMAS)
            dve.wait_ge(s["pool_step"], 8)
            link(dve.tensor_copy(lens[:, :], lens_i[:, :]))
            dve.tensor_scalar(w_lo[:, :], pt[:, :], -WINDOW, 0.0, ALU.add, ALU.max)
            link(dve.tensor_scalar(w_hi[:, :], pt[:, :], WINDOW, None, ALU.add))
            link(dve.tensor_tensor(w_hi[:, :], w_hi[:, :], lens[:, :], ALU.min))
            for i in range(3):
                for j in range(NJ):
                    dve.tensor_scalar(q_bias[i][:, j, :], tau[:, :], bqs[i][:, j:j + 1], special[:, NJ:NJ + 1], ALU.mult, ALU.subtract)
                last = dve.tensor_tensor(k_bias[i][:, :], bks[i][:, :], special[:, 0:NJ], ALU.add)
            link(last)
            for q in range(PREPS):
                dve.wait_ge(s["prep_ps"], q + 1)
                bank = psS[:, q % 4, :]
                if q < NB // 4:
                    last = dve.tensor_copy(tiles(ctxT[:, q * GK:(q + 1) * GK]), tiles(bank)[:, :, 0:KEYS])
                else:
                    for c in range(4):
                        n = 4 * q + c
                        src = bank[:, c * P:c * P + rows_of[n]]
                        if n == 16:
                            dst = waT[:, :]
                        elif n < 19:
                            dst = wcT[:, n - 17, :]
                        elif n < 31:
                            i, m = divmod(n - 19, 4)
                            dst = (wq[i], wk[i], wvT[i], woT[i])[m][:, :]
                            if m < 2:
                                dst = dst.rearrange("p (h c) -> p h c", c=ROW)[:, :, 0:HD]
                                src = src.rearrange("p (h c) -> p h c", c=HD)
                        elif n < 39:
                            dst = geT[:, (n - 31) * P:(n - 30) * P]
                        elif n < 47:
                            dst = upT[:, (n - 39) * P:(n - 38) * P]
                        elif n < 49:
                            dst = geT[:, (n - 47 + 8) * P:(n - 46 + 8) * P]
                        elif n < 51:
                            dst = upT[:, (n - 49 + 8) * P:(n - 48 + 8) * P]
                        elif n < 61:
                            dst = dnT[:, n - 51, :]
                        else:
                            dst = (r1, r3, b1T)[n - 61][:, :]
                        last = dve.tensor_copy(dst, src)
                last.then_inc(s["prep_sb"], 1)
            dve.wait_ge(s["x_in"], 16)

            def layer_norm(n, src, done=None, scale=None):
                for b in range(GB):
                    last = dve.bn_stats(stats[:, b, :], src(b))
                link(last, alone=True)
                for b in range(GB):
                    last = dve.bn_aggr(mv[:, b, :], stats[:, b, :])
                last.then_inc(s["ln_var"], 1)
                dve.wait_ge(s["ln_rstd"], n + 1)
                r = rstd
                if scale is not None:
                    link(dve.tensor_tensor(rstd_t[:], rstd[:], scale, ALU.mult))
                    r = rstd_t
                for b in range(GB):
                    last = dve.tensor_scalar(tok(xn, b), src(b), mv[:, b, 0:1], r[:, b:b + 1], ALU.subtract, ALU.mult)
                if done:
                    last.then_inc(s[done], 1)
                else:
                    link(last)

            def bcast(small2d, n):
                return small2d.unsqueeze(2).broadcast_to([small2d.shape[0], small2d.shape[1], n])

            def over(ap2d, n):
                return ap2d.unsqueeze(1).broadcast_to([ap2d.shape[0], n, ap2d.shape[1]])

            def window_attention(g):
                layer_norm(g, lambda b: x_tile(g, b), done="xn_ready")
                keep, gauss, sc, pen = tmp[:, 0:GK], tmp2[:, 0:GK], probs[:, 0:GK], hT[0][:, 0, 0:GK]
                pos = over(iota[:, 0:KEYS], GB)
                grp = bass.ds(g * GB, GB)
                dve.tensor_tensor(tiles(keep), pos, bcast(w_lo[:, grp], KEYS), ALU.is_ge)
                link(dve.tensor_tensor(tiles(gauss), pos, bcast(w_hi[:, grp], KEYS), ALU.is_le))
                link(dve.tensor_tensor(keep, keep, gauss, ALU.mult))
                link(dve.tensor_tensor(tiles(gauss), pos, bcast(pt[:, grp], KEYS), ALU.subtract))
                dve.tensor_tensor(gauss, gauss, gauss, ALU.mult).then_inc(s["gauss_arg"], 1)
                link(dve.tensor_scalar(pen, keep, MASKED, -MASKED, ALU.mult, ALU.add))
                dve.wait_ge(s["score_ps"], g + 1)
                link(dve.tensor_tensor(sc, psS[:, 0, 0:GK], keep, ALU.mult))
                link(dve.tensor_tensor(sc, sc, pen, ALU.add))
                link(dve.reduce_max(gap[:, :], tiles(sc), AX_X))
                dve.tensor_tensor(tiles(sc), tiles(sc), bcast(gap[:, :], KEYS), ALU.subtract).then_inc(s["x0_shifted"], 1)
                dve.wait_ge(s["x0_exp_ready"], g + 1)
                link(dve.reduce_sum(w1[:, :], tiles(sc), AX_X))
                link(dve.reciprocal(w2[:, :], w1[:, :]))
                dve.wait_ge(s["gauss_ready"], g + 1)
                for b in range(GB):
                    last = dve.scalar_tensor_tensor(tiles(sc)[:, b, :], tiles(sc)[:, b, :], w2[:, b:b + 1],
                                                    tiles(gauss)[:, b, :], ALU.mult, ALU.mult)
                last.then_inc(s["align_ready"], 1)
                dve.wait_ge(s["tanh_ready"], g + 1)
                link(dve.tensor_tensor(x_group(g), x_group(g), tmp[:, :], ALU.add))

            def attention(i, g):
                a = i * NG + g
                grp = bass.ds(g * GB, GB)
                layer_norm(LN_OF[2 * i + 2] + g, lambda b: x_tile(g, b), done="xn_ready", scale=tau[:, grp])
                for j in range(NJ):
                    dve.wait_ge(s["k_ps"], a * NJ + j + 1)
                    dve.scalar_tensor_tensor(ks[:, j, :], psH[:, j % 2, 0:GK], k_bias[i][:, j:j + 1],
                                             deltaK[:, bass.ds(g * GK, GK)], ALU.add, ALU.add).then_inc(s["k_ready"], 1)
                dve.wait_ge(s["v_ps"], a + 1)
                for b in range(GB):
                    last = dve.tensor_tensor(vaug[:, b, :, 0:HD], psY[0:KEYS, b * P:(b + 1) * P].rearrange("p (h c) -> p h c", c=HD),
                                             bv[i][0:KEYS, :].rearrange("p (h c) -> p h c", c=HD), ALU.add)
                last.then_inc(s["v_ready"], 1)
                for j in range(NJ):
                    dve.wait_ge(s["q_ps"], a * NJ + j + 1)
                    dve.tensor_tensor(tiles(qs[:, j, :]), tiles(psH[:, j % 2, :]), bcast(q_bias[i][:, j, grp], P),
                                      ALU.add).then_inc(s["q_ready"], 1)
                for b in range(GB):
                    n = a * GB + b
                    dve.wait_ge(s["a_ps"], n + 1)
                    m_out = m_pad[:, :].rearrange("p (r c) -> p r c", c=ROW)[:, :, M_ROW:M_ROW + NJ]
                    dve.reduce_max(m_out, psS[:, :, 0:GK].rearrange("p r (j k) -> p r j k", k=KEYS), AX_X).then_inc(s["max_ready"], 1)
                    dve.wait_ge(s["maxT_ps"], n + 1)
                    qb = qs[:, :, b * P:(b + 1) * P]
                    dve.tensor_tensor(qb, qb, over(psM[:, 0:P], NJ), ALU.add).then_inc(s["q_shifted"], 1)
                    dve.wait_ge(s["o_ps"], n + 1)
                    ob = psY[:, 0:H * (HD + 1)].rearrange("p (h c) -> p h c", c=HD + 1)
                    link(dve.reciprocal(rden[:, b, :], ob[:, :, HD]))
                    dve.tensor_tensor(tok(attn, b).rearrange("p (h c) -> p h c", c=HD), ob[:, :, 0:HD], bcast(rden[:, b, :], HD),
                                      ALU.mult).then_inc(s["attn_ready"], 1)
                dve.wait_ge(s["wo_ps"], a + 1)
                dve.tensor_tensor(x_group(g), x_group(g), psH[:, 0, :], ALU.add).then_inc(s["x_done"], 1)
                dve.wait_ge(s["x_done"], a + 1)
                link(dve.tensor_tensor(tiles(x_group(g)), tiles(x_group(g)), over(bo[i][:, :], GB), ALU.add))

            def route(f, n_e, width, bias):
                dve.wait_ge(s["logits_ps"], f + 1)
                ps = psM[:, 0:GB * width].rearrange("p (b e) -> p b e", e=width)
                if bias is None:
                    link(dve.tensor_copy(lg[:, :, 0:width], ps), alone=True)
                else:
                    link(dve.tensor_tensor(lg[:, :, 0:width], ps, over(bias[:, :], GB), ALU.add), alone=True)
                for b in range(GB):
                    last = dve.max(mx[:, b, :], lg[:, b, 0:n_e])
                link(last)
                dve.tensor_tensor(gap[:, :], mx[:, :, 0], mx[:, :, 1], ALU.subtract).then_inc(s["gap_ready"], 1)
                for b in range(GB):
                    last = dve.max_index(ix[:, b, :], mx[:, b, :], lg[:, b, 0:n_e])
                link(last)
                link(dve.tensor_copy(ixf[:, :, :], ix[:, :, 0:2]))
                pos = over(iota[:, 0:n_e], GB)
                first, second = oh1[:, :, 0:n_e], oh2[:, :, 0:n_e]
                dve.tensor_tensor(first, pos, bcast(ixf[:, :, 0], n_e), ALU.is_equal)
                dve.tensor_tensor(second, pos, bcast(ixf[:, :, 1], n_e), ALU.is_equal)
                dve.wait_ge(s["gate_ready"], f + 1)
                dve.tensor_scalar(w1[:, :], th[:, :], 0.5, 0.5, ALU.mult, ALU.add)
                link(dve.tensor_scalar(w2[:, :], th[:, :], -0.5, 0.5, ALU.mult, ALU.add))
                dve.tensor_tensor(first, first, bcast(w1[:, :], n_e), ALU.mult)
                link(dve.tensor_tensor(second, second, bcast(w2[:, :], n_e), ALU.mult))
                if width > n_e:
                    dve.tensor_scalar(comb[:, :, n_e], ths[:, :], 0.5, 0.5, ALU.mult, ALU.add)
                dve.tensor_tensor(comb[:, :, 0:n_e], first, second, ALU.add).then_inc(s["comb_ready"], 1)

            def moe(li, g, bias, has_b2):
                f, m = MOE_F[li] * NG + g, li * NG + g
                ln = LN_OF[MOE_FRONT[li]] + (2 * g if li == 0 else g)
                layer_norm(ln, lambda b: x_tile(g, b), done="xn_ready")
                route(f, E8, E8, bias)
                acc = (lambda b: tok(xn, b)) if li == 0 else (lambda b: x_tile(g, b))
                acc_all = xn[:, :] if li == 0 else x_group(g)
                if has_b2:
                    dve.wait_ge(s["b2_ps"], m + 1)
                    dve.tensor_tensor(acc_all, acc_all, psY[:, :], ALU.add).then_inc(s["b2_added"], 1)
                    dve.wait_ge(s["b2_added"], m + 1)
                for e in range(E8):
                    if e:
                        dve.wait_ge(s["y_added"], m * E8 + e)
                    dve.wait_ge(s["y_ps"], m * E8 + e + 1)
                    for b in range(GB):
                        last = dve.scalar_tensor_tensor(acc(b), tok(psY, b), comb[:, b, e:e + 1], acc(b), ALU.mult, ALU.add)
                    last.then_inc(s["y_added"], 1)
                dve.wait_ge(s["y_added"], m * E8 + E8)
                if li == 0:
                    layer_norm(ln + 1, lambda b: tok(xn, b))
                    link(dve.tensor_tensor(tiles(xn[:, :]), tiles(xn[:, :]), over(gamma[:, :], GB), ALU.mult))
                    link(dve.tensor_tensor(tiles(xn[:, :]), tiles(xn[:, :]), over(beta[:, :], GB), ALU.add))
                    link(dve.tensor_tensor(x_group(g), x_group(g), xn[:, :], ALU.add))

            def gated(g):
                layer_norm(LN_OF[3] + g, lambda b: x_tile(g, b), done="xn_ready")
                route(NG + g, E16, E16 + 1, None)
                for c in range(CH1):
                    n = g * CH1 + c
                    dve.wait_ge(s["silu_ready"], n + 1)
                    link(dve.tensor_tensor(hT[c % 2][:, 1, :], hT[c % 2][:, 0, :], weight_bank(c), ALU.mult))
                    if c >= 2:
                        dve.wait_ge(s["f1_down"], n - 1)
                    dve.tensor_tensor(hT[c % 2][:, 2, :], hT[c % 2][:, 1, :], up_bank(c), ALU.mult).then_inc(s["f1_h_ready"], 1)
                dve.wait_ge(s["f1_y_ps"], g + 1)
                link(dve.tensor_tensor(x_group(g), x_group(g), psM[:, :], ALU.add))

            stage("x0", window_attention)
            stage("f0", lambda g: moe(0, g, rb0, True))
            stage("x", lambda g: attention(0, g))
            stage("f1", gated)
            stage("x", lambda g: attention(1, g))
            stage("f2", lambda g: moe(1, g, rb2, True))
            stage("x", lambda g: attention(2, g))
            stage("f3", lambda g: moe(2, g, None, False))

        @block.tensor
        def _(pe):
            pe.wait_ge(s["nat_in"], 16 * NAT_DMAS)
            pe.wait_ge(s["consts_ready"], 4)
            for q in range(PREPS):
                if q >= 4:
                    pe.wait_ge(s["prep_sb"], q - 3)
                for c in range(4):
                    n = 4 * q + c
                    rows = rows_of[n]
                    last = pe.transpose(psS[:, q % 4, c * P:c * P + rows], nat[0:rows, n, :], ident[0:rows, 0:rows])
                last.then_inc(s["prep_ps"], 1)
            pe.wait_ge(s["prep_sb"], PREPS)
            pe.wait_ge(s["small_in"], 16 * SMALL_DMAS)

            def mm(o, l, r, start=True, stop=True, **kw):
                return pe.matmul(o, l, r, start=start, stop=stop, **kw)

            def front(n):
                pe.wait_ge(s["xn_ready"], n + 1)
                for b in range(GB):
                    last = pe.transpose(tok(psM, b), tok(xn, b), ident[:, :])
                last.then_inc(s["xnT_ps"], 1)
                pe.wait_ge(s["xnT_ready"], n + 1)

            def window_attention(g):
                mm(psH[:, 0, 0:GK], waT[:, :], ctxT[:, bass.ds(g * GK, GK)]).then_inc(s["wa_ps"], 1)
                front(g)
                pe.wait_ge(s["wa_ready"], g + 1)
                for b in range(GB):
                    last = mm(psS[:, 0, b * KEYS:(b + 1) * KEYS], tok(xnT, b), attn[:, b * KEYS:(b + 1) * KEYS])
                last.then_inc(s["score_ps"], 1)
                pe.wait_ge(s["align_ready"], g + 1)
                for b in range(GB):
                    last = pe.transpose(psM[0:KEYS, b * P:(b + 1) * P], probs[:, b * KEYS:(b + 1) * KEYS], ident[:, :])
                last.then_inc(s["alignT_ps"], 1)
                pe.wait_ge(s["alignT_ready"], g + 1)
                pe.wait_ge(s["ctx_g_in"], g * 16 + 16)
                for b in range(GB):
                    last = mm(tok(psY, b), ctx_g[:, b, :], probs[0:KEYS, 1024 + b * P:1024 + (b + 1) * P])
                last.then_inc(s["context_ps"], 1)
                pe.wait_ge(s["context_ready"], g + 1)
                for b in range(GB):
                    mm(psH[:, 1, b * P:(b + 1) * P], tok(attnT, b), wcT[:, 0, :], stop=False)
                    last = mm(psH[:, 1, b * P:(b + 1) * P], tok(xnT, b), wcT[:, 1, :], start=False)
                last.then_inc(s["mix_ps"], 1)

            def attention(i, g):
                a = i * NG + g
                front((2 * i + 2) * NG + g)
                for j in range(NJ):
                    if j >= 2:
                        pe.wait_ge(s["k_ready"], a * NJ + j - 1)
                    mm(psH[:, j % 2, 0:GK], wk[i][:, j * P:(j + 1) * P], ctxT[:, bass.ds(g * GK, GK)]).then_inc(s["k_ps"], 1)
                pe.wait_ge(s["ctxT_g_in"], a * 16 + 16)
                for b in range(GB):
                    last = mm(psY[0:KEYS, b * P:(b + 1) * P], ctxT_g[:, b * KEYS:(b + 1) * KEYS], wvT[i][:, :])
                last.then_inc(s["v_ps"], 1)
                pe.wait_ge(s["k_ready"], a * NJ + NJ)
                for j in range(NJ):
                    if j >= 2:
                        pe.wait_ge(s["q_ready"], a * NJ + j - 1)
                    mm(psH[:, j % 2, :], wq[i][:, j * P:(j + 1) * P], xnT[:, :]).then_inc(s["q_ps"], 1)
                pe.wait_ge(s["q_ready"], a * NJ + NJ)
                pe.wait_ge(s["v_ready"], a + 1)
                for b in range(GB):
                    n = a * GB + b
                    if b:
                        pe.wait_ge(s["probs_ready"], n)
                    for j in range(NJ):
                        for r in range(4):
                            rr = slice(ROW * r, ROW * r + ROW)
                            last = mm(psS[:, r, j * KEYS:(j + 1) * KEYS], qs[rr, j, b * P:(b + 1) * P], ks[rr, j, b * KEYS:(b + 1) * KEYS])
                    last.then_inc(s["a_ps"], 1)
                    pe.wait_ge(s["max_ready"], n + 1)
                    pe.transpose(psM[:, 0:P], m_pad[:, :], ident[:, :]).then_inc(s["maxT_ps"], 1)
                    pe.wait_ge(s["q_shifted"], n + 1)
                    for j in range(NJ):
                        for r in range(4):
                            rr = slice(ROW * r, ROW * r + ROW)
                            last = mm(psS[0:KEYS, r, j * P:(j + 1) * P], ks[rr, j, b * KEYS:(b + 1) * KEYS], qs[rr, j, b * P:(b + 1) * P])
                    last.then_inc(s["b_ps"], 1)
                    pe.wait_ge(s["probs_ready"], n + 1)
                    if b:
                        pe.wait_ge(s["attn_ready"], n)
                    for h in range(H):
                        j, r = divmod(h, 4)
                        last = mm(psY[:, h * (HD + 1):(h + 1) * (HD + 1)], probs[0:KEYS, r * 512 + j * P:r * 512 + (j + 1) * P], vaug[:, b, h, :])
                    last.then_inc(s["o_ps"], 1)
                pe.wait_ge(s["attn_ready"], a * GB + GB)
                for b in range(GB):
                    last = pe.transpose(psH[:, 1, b * P:(b + 1) * P], tok(attn, b), ident[:, :])
                last.then_inc(s["attnT_ps"], 1)
                pe.wait_ge(s["attnT_ready"], a + 1)
                for b in range(GB):
                    last = mm(psH[:, 0, b * P:(b + 1) * P], tok(attnT, b), woT[i][:, :])
                last.then_inc(s["wo_ps"], 1)

            def logits(router, width):
                for b in range(GB):
                    last = mm(psM[:, b * width:(b + 1) * width], tok(xnT, b), router[:, 0:width])
                last.then_inc(s["logits_ps"], 1)

            def comb_transposed(f, width):
                pe.wait_ge(s["comb_ready"], f + 1)
                for b in range(GB):
                    last = pe.transpose(psM[0:width, b * P:(b + 1) * P], comb[:, b, 0:width], ident[:, :])
                last.then_inc(s["combT_ps"], 1)

            def moe(li, g, home, router, b2):
                f, m = MOE_F[li] * NG + g, li * NG + g
                wi, wo = w1_of(home), w2_of(home)
                front(MOE_FRONT[li] * NG + g)
                logits(router, E8)

                def first(e, ks=range(HC)):
                    for k in ks:
                        c = e * HC + k
                        if c >= 2:
                            pe.wait_ge(s["h_ready"], m * (E8 * HC) + c - 1)
                        mm(psH[:, c % 2, :], wi[:, e * HID + k * P:e * HID + (k + 1) * P], xnT[:, :]).then_inc(s["h_ps"], 1)

                first(0, (0, 1))
                comb_transposed(f, E8)
                pe.wait_ge(s["combT_ready"], f + 1)
                if b2 is not None:
                    for b in range(GB):
                        last = mm(tok(psY, b), combT[0:E8, b * P:(b + 1) * P], b2[:, :])
                    last.then_inc(s["b2_ps"], 1)
                first(0, (2, 3))
                for e in range(E8):
                    if e + 1 < E8:
                        first(e + 1)
                    pe.wait_ge(s["h_ready"], m * (E8 * HC) + (e + 1) * HC)
                    if e:
                        pe.wait_ge(s["y_added"], m * E8 + e)
                    elif b2 is not None:
                        pe.wait_ge(s["b2_added"], m + 1)
                    for b in range(GB):
                        for k in range(HC):
                            last = mm(tok(psY, b), hT[e % 2][:, k, b * P:(b + 1) * P], wo[:, e, k, :], start=k == 0, stop=k == HC - 1)
                    last.then_inc(s["y_ps"], 1)

            def gated(g):
                f = NG + g
                front(3 * NG + g)
                logits(r1, E16 + 1)
                comb_transposed(f, E16 + 1)
                pe.wait_ge(s["combT_ready"], f + 1)

                def down(c):
                    pe.wait_ge(s["f1_h_ready"], g * CH1 + c + 1)
                    mm(psY[:, :], dnT[:, c, :], hT[c % 2][:, 2, :], start=c == 0, stop=c == CH1 - 1).then_inc(s["f1_down"], 1)

                for c in range(CH1):
                    if c >= 2:
                        pe.wait_ge(s["f1_h_ready"], g * CH1 + c - 1)
                    mm(gate_bank(c), geT[:, c * P:(c + 1) * P], xnT[:, :])
                    mm(up_bank(c), upT[:, c * P:(c + 1) * P], xnT[:, :])
                    mm(weight_bank(c), sel[:, c * P:(c + 1) * P], combT[:, :]).then_inc(s["f1_ps"], 1)
                    if c:
                        down(c - 1)
                down(CH1 - 1)
                pe.wait_ge(s["f1_yT_ready"], g + 1)
                for b in range(GB):
                    last = pe.transpose(tok(psM, b), tok(attnT, b), ident[:, :])
                last.then_inc(s["f1_y_ps"], 1)

            with pe.Fori(0, NG) as g:
                window_attention(g)
            pe.wait_ge(s["moeA_in"], 16 * MOE_DMAS)
            with pe.Fori(0, NG) as g:
                moe(0, g, moeA, r0, b2_0)
            with pe.Fori(0, NG) as g:
                attention(0, g)
            with pe.Fori(0, NG) as g:
                gated(g)
            with pe.Fori(0, NG) as g:
                attention(1, g)
            pe.wait_ge(s["moeB_in"], 16 * MOE_DMAS)
            with pe.Fori(0, NG) as g:
                moe(1, g, moeB, r2, b2_2)
            with pe.Fori(0, NG) as g:
                attention(2, g)
            pe.wait_ge(s["moeA_in"], 2 * 16 * MOE_DMAS)
            with pe.Fori(0, NG) as g:
                moe(2, g, moeA, r3, None)


def kernel(**inputs):
    import numpy as _np
    import concourse.bacc as _bacc
    from concourse import mybir as _mybir
    from concourse.bass_utils import run_bass_kernel_spmd as _run

    nc = _bacc.Bacc("TRN2", target_bir_lowering=False, num_devices=1)
    arrays, t = {}, {}
    for name, value in inputs.items():
        a = _np.ascontiguousarray(value)
        arrays[f"in_{name}"] = a
        t[name] = nc.dram_tensor(f"in_{name}", a.shape, _mybir.dt.from_np(a.dtype), kind="ExternalInput").ap()
    out = nc.dram_tensor("out_x", inputs["x"].shape, _mybir.dt.float32, kind="ExternalOutput").ap()
    build(nc, t, out)
    r = _run(nc, [arrays], core_ids=[0])
    return r.results[0]["out_x"]
```

```python
from contextlib import ExitStack

import concourse.bass as bass
from concourse import mybir

F32 = mybir.dt.float32
I32 = mybir.dt.int32
U32 = mybir.dt.uint32
ALU = mybir.AluOpType
ACT = mybir.ActivationFunctionType
AX_X = mybir.AxisListType.X

P = 128
NB = 16
GB = 4
NG = NB // GB
GT = GB * P
KEYS = 120
GK = GB * KEYS
H, HD = 16, 8
ROW = 32
NJ = 4
M_ROW = 24
D_ROW = 28
E8, HID, HC = 8, 512, 4
E16, CH1 = 16, 10
LN_EPS = 1e-5
WINDOW, DEV_POW = 16.0, 128.0
MASKED = 1.0e9
SCALE = float(HD) ** -0.5

LINKS = {"f0x0": 23, "f0x1": 0, "f1x1": 15, "f1x2": 0, "f2x2": 14, "f2x3": 0, "f3x3": 14, "f3": 0}

LN_BASE, LN_PER = [1, 3 * NG + 1, 5 * NG + 1, 7 * NG + 1], [3, 2, 2, 2]
LN_TOTAL = 9 * NG
MOE_OF = {0: 0, 2: 1, 3: 2}


def merged(experts, attention, spare=3):
    order, sent = [], 0
    for n, part in enumerate(experts):
        order.append(("experts", part))
        due = min(len(attention), -(-(n + 1) * len(attention) // (len(experts) - spare)))
        order += [("attention", p) for p in attention[sent:due]]
        sent = due
    return order


WINDOW_PARTS = [("scores",), ("align",), ("context",), ("mix",)]
HEADS_PARTS = ([("keys",), ("front",), ("values",), ("queries",)]
               + [(part, b) for b in range(GB) for part in ("maxima", "shift", "scores", "output", "divide")]
               + [("transpose",), ("project",)])
MOE_PARTS = [("front",), ("route",), ("hidden", 0, 1)]
for _e in range(E8):
    if _e + 1 < E8:
        MOE_PARTS += [("hidden", _e + 1, 0), ("hidden", _e + 1, 1)]
    MOE_PARTS += [("out", _e)]
MOE_PARTS += [("end",)]
GATED_PARTS = [("front",), ("route",)] + [(part, c) for c in range(CH1) for part in ("hidden", "weigh", "out")] + [("end",)]


def pair_rows(w):
    return w.rearrange("e h d -> (e h) d").rearrange("(c a) d -> a c d", a=P)


def build(nc, t, out):
    ctx = ExitStack()
    with ctx:
        def sb(name, shape, dt=F32):
            return ctx.enter_context(nc.sbuf_tensor(name, shape, dt))

        def sem(name):
            return ctx.enter_context(nc.semaphore(name))

        x = sb("x", [P, NB * P])
        xa = sb("xa", [P, GT])
        xaT = sb("xaT", [P, GT])
        xn = sb("xn", [P, GT])
        xnT = sb("xnT", [P, GT])
        ctxT = sb("ctxT", [P, NB * KEYS])
        ctxT_g = sb("ctxT_g", [P, GK])
        ident = sb("ident", [P, P])
        wq = [sb(f"wq{i}", [P, H * ROW]) for i in range(3)]
        wk = [sb(f"wk{i}", [P, H * ROW]) for i in range(3)]
        wvT = [sb(f"wvT{i}", [P, P]) for i in range(3)]
        woT = [sb(f"woT{i}", [P, P]) for i in range(3)]
        bv = [sb(f"bv{i}", [P, P]) for i in range(3)]
        bo = [sb(f"bo{i}", [P, P]) for i in range(3)]
        bqs = [sb(f"bqs{i}", [P, NJ]) for i in range(3)]
        bks = [sb(f"bks{i}", [P, NJ]) for i in range(3)]
        q_bias = [sb(f"q_bias{i}", [P, NJ, NB]) for i in range(3)]
        k_bias = [sb(f"k_bias{i}", [P, NJ]) for i in range(3)]
        special = sb("special", [P, NJ + 1])
        deltaK = sb("deltaK", [P, NB * KEYS])
        waT = sb("waT", [P, P])
        wcT = sb("wcT", [P, 2, P])
        moeA = sb("moeA", [P, 2 * E8 * HID])
        moeB = sb("moeB", [P, 2 * E8 * HID])
        nat = moeB[:, :].rearrange("p (s c) -> p s c", c=P)
        geT = sb("geT", [P, CH1 * P])
        upT = sb("upT", [P, CH1 * P])
        dnT = sb("dnT", [P, CH1, P])
        r0 = sb("r0", [P, E8])
        r1 = sb("r1", [P, E16 + 1])
        r2 = sb("r2", [P, E8])
        r3 = sb("r3", [P, E8])
        rb0 = sb("rb0", [P, E8])
        rb2 = sb("rb2", [P, E8])
        b1T = sb("b1T", [P, 2 * E8 * HC])
        b2_0 = sb("b2_0", [E8, P])
        b2_2 = sb("b2_2", [E8, P])
        gamma = sb("gamma", [P, P])
        beta = sb("beta", [P, P])
        tau = sb("tau", [P, NB])
        pt = sb("pt", [P, NB])
        lens_i = sb("lens_i", [P, NB], I32)
        lens = sb("lens", [P, NB])
        w_lo = sb("w_lo", [P, NB])
        w_hi = sb("w_hi", [P, NB])
        iota_i = sb("iota_i", [P, P], I32)
        iota = sb("iota", [P, P])
        half = sb("half", [P, GB])
        sel = sb("sel", [E16 + 1, CH1 * P])
        stats = sb("stats", [P, GB, 6])
        mv = sb("mv", [P, GB, 2])
        vpe = sb("vpe", [P, GB])
        rstd = sb("rstd", [P, GB])
        rstd_t = sb("rstd_t", [P, GB])
        qs = sb("qs", [P, NJ, GT])
        ks = sb("ks", [P, NJ, GK])
        vaug = sb("vaug", [KEYS, GB, H, HD + 1])
        probs = sb("probs", [P, 4 * 512])
        m_pad = sb("m_pad", [P, P])
        rden = sb("rden", [P, GB, H])
        top = sb("top", [P, GB])
        den = sb("den", [P, GB])
        inv = sb("inv", [P, GB])
        attn = sb("attn", [P, GT])
        attnT = sb("attnT", [P, GT])
        kbd = sb("kbd", [P, 2, NJ, 4, KEYS])
        row_block = sb("row_block", [P, 4])
        flat = kbd[:, :, :, :, :].rearrange("p b j r k -> p (b j r k)")
        tmp, tmp2 = flat[:, 0:GT], flat[:, GT:2 * GT]
        ctx_g = flat[0:KEYS, 2 * GT:3 * GT].rearrange("p (b c) -> p b c", b=GB)
        lg = sb("lg", [P, GB, E16 + 1])
        mx = sb("mx", [P, GB, 8])
        ix = sb("ix", [P, GB, 8], U32)
        ixf = sb("ixf", [P, GB, 2])
        oh1 = sb("oh1", [P, GB, E16])
        oh2 = sb("oh2", [P, GB, E16])
        gap = sb("gap", [P, GB])
        th = sb("th", [P, GB])
        ths = sb("ths", [P, GB])
        w1 = sb("w1", [P, GB])
        w2 = sb("w2", [P, GB])
        comb = sb("comb", [P, GB, E16 + 1])
        combT = sb("combT", [E16 + 1, GT])
        hT = [sb(f"hT{i}", [P, HC, GT]) for i in range(2)]

        psS = ctx.enter_context(nc.psum_tensor("psS", [P, 4, 512], F32))
        psH = ctx.enter_context(nc.psum_tensor("psH", [P, 2, 512], F32))
        psY = ctx.enter_context(nc.psum_tensor("psY", [P, 512], F32))
        psM = ctx.enter_context(nc.psum_tensor("psM", [P, 512], F32))

        names = """x_in nat_in small_in moeA_in moeB_in ctx_g_in ctxT_g_in out_done
            zeroed consts_ready pool_step prep_ps prep_sb vec_step tables_ready
            ln_var ln_vpe ln_rstd xn_ready xnT_ps xnT_ready xa_ready xaT_ps xaT_ready
            wa_ps wa_ready score_ps gauss_arg gauss_ready x0_shifted x0_exp_ready align_ready alignT_ps alignT_ready
            context_ps context_ready mix_ps tanh_ready x0_done
            k_ps k_ready kbd_ready v_ps v_ready q_ps q_ready a_ps max_ready maxT_ps q_shifted b_ps probs_ready o_ps oT_ready on_ps attn_ready
            attnT_ps attnT_ready wo_ps x_done
            logits_ps gap_ready gate_ready comb_ready combT_ps combT_ready b2_ps b2_added
            h_ps h_ready y_ps y_added f0_done
            f1_ps silu_ready f1_t_ready f1_w_ps f1_h_ready f1_down f1_yT_ready f1_y_ps f1_done""".split()
        s = {n: sem(n) for n in names}

        def bc_row(row, n):
            return row.rearrange("(a n) -> a n", a=1).broadcast_to([P, n])

        def tok(buf, b=0, n=1):
            return buf[:, b * P:(b + n) * P]

        def tiles(ap2d, n=GB):
            return ap2d.rearrange("p (b c) -> p b c", b=n)

        def x_tile(g, b):
            return x[:, bass.ds(g * GT + b * P, P)]

        def x_group(g):
            return x[:, bass.ds(g * GT, GT)]

        def w1_of(home):
            return home[:, 0:E8 * HID]

        def w2_of(home):
            return home[:, E8 * HID:].rearrange("p (e k d) -> p e k d", e=E8, k=HC)

        SLOTS = 64
        rows_of = [KEYS] * NB + [P] * (SLOTS - NB)
        rows_of[61], rows_of[62], rows_of[63] = E16 + 1, E8, 2 * E8 * HC
        NAT_DMAS, SMALL_DMAS, MOE_DMAS = 26, 17 + 4 * 7, 1 + E8
        PREPS = SLOTS // 4

        def attention_norm(i, g):
            if i == 0 and isinstance(g, int):
                return 0
            if isinstance(g, int):
                return LN_BASE[i - 1] + LN_PER[i - 1] * (NG - 1) + 1
            return LN_BASE[i] + LN_PER[i] * (g - 1) + 1

        def steps(eng, window, heads, moe, gated):
            for part in WINDOW_PARTS:
                window(0, 0, part)
            for i in range(4):
                experts, parts = (gated, GATED_PARTS) if i == 1 else (moe, MOE_PARTS)
                beside, names = (window, WINDOW_PARTS) if i == 0 else (heads, HEADS_PARTS)
                if i != 1:
                    yield ("load", None, i)
                with eng.Fori(0, NG - 1) as g:
                    yield ("begin", f"f{i}x{i}", g)
                    for who, part in merged(parts, names):
                        if who == "experts":
                            experts(i, g, part)
                        else:
                            beside(i, g + 1, part)
                    yield ("end", f"f{i}x{i}", g)
                yield ("once", None, None)
                for who, part in merged(parts, HEADS_PARTS if i < 3 else []):
                    if who == "experts":
                        experts(i, NG - 1, part)
                    else:
                        heads(i + 1, 0, part)

        block = ctx.enter_context(nc.Block())

        @block.sync
        def _(sp):
            count = [0]

            def nat_load(dst, src):
                count[0] += 1
                sp.dma_start(dst, src).then_inc(s["nat_in"], 16)

            def moe_load(home, w1d, w2d, done):
                sp.dma_start(w1_of(home).rearrange("p (e h) -> p e h", e=E8), w1d.rearrange("e d h -> d e h")).then_inc(done, 16)
                for e in range(E8):
                    sp.dma_start(w2_of(home)[:, e], w2d[e].rearrange("(k p) d -> p k d", k=HC)).then_inc(done, 16)

            nat_load(nat[0:KEYS, 0:NB, :], t["ctx_1024"].rearrange("b k d -> k b d"))
            nat_load(nat[:, 16, :], t["L0_xcond_W_a"])
            nat_load(nat[:, 17:19, :], t["L0_xcond_W_c"].rearrange("o (h k) -> o h k", h=2))
            sp.dma_start(tiles(x[:, :], NB), t["x"].rearrange("b p d -> p b d")).then_inc(s["x_in"], 16)
            for i in range(3):
                for m, w in enumerate("qkvo"):
                    nat_load(nat[:, 19 + 4 * i + m, :], t[f"L{i + 1}_xcond_W{w}"])
            nat_load(nat[:, 31:39, :], pair_rows(t["L1_ffn_We_gate"]))
            nat_load(nat[:, 39:47, :], pair_rows(t["L1_ffn_We_up"]))
            nat_load(nat[:, 47:49, :], t["L1_ffn_Ws_gate"].rearrange("(c h) d -> h c d", c=2))
            nat_load(nat[:, 49:51, :], t["L1_ffn_Ws_up"].rearrange("(c h) d -> h c d", c=2))
            nat_load(nat[:, 51:59, :].rearrange("p c (a h) -> p (c a) h", a=2), t["L1_ffn_We_down"].rearrange("e d h -> d e h"))
            nat_load(nat[:, 59:61, :], t["L1_ffn_Ws_down"].rearrange("d (c h) -> d c h", c=2))
            nat_load(nat[0:E16, 61, :], t["L1_ffn_Wg"])
            nat_load(nat[E16:E16 + 1, 61, :], t["L1_ffn_Wsg"])
            nat_load(nat[0:E8, 62, :], t["L3_ffn_router_w"])
            nat_load(nat[0:32, 63, :], t["L0_ffn_b1"].rearrange("e (k p) -> (e k) p", k=HC))
            nat_load(nat[32:64, 63, :], t["L2_ffn_b1"].rearrange("e (k p) -> (e k) p", k=HC))
            assert count[0] == NAT_DMAS, count
            moe_load(moeA, t["L0_ffn_W1"], t["L0_ffn_W2"], s["moeA_in"])
            sp.dma_start(ctx_g[:, :, :], t["ctx_1024"][0:GB].rearrange("b k d -> k b d")).then_inc(s["ctx_g_in"], 16)
            with sp.Fori(1, NG) as g:
                sp.wait_ge(s["context_ps"], g)
                sp.dma_start(ctx_g[:, :, :], t["ctx_1024"][bass.ds(g * GB, GB)].rearrange("b k d -> k b d")).then_inc(s["ctx_g_in"], 16)
            sp.wait_ge(s["prep_ps"], PREPS)
            moe_load(moeB, t["L2_ffn_W1"], t["L2_ffn_W2"], s["moeB_in"])
            sp.wait_ge(s["prep_sb"], PREPS)
            for i in range(3):
                if i == 0:
                    sp.dma_start(ctxT_g[:, :], ctxT[:, 0:GK]).then_inc(s["ctxT_g_in"], 16)
                    sp.wait_ge(s["y_added"], NG * E8)
                    moe_load(moeA, t["L3_ffn_w1"], t["L3_ffn_w2"], s["moeA_in"])
                with sp.Fori(1 if i == 0 else 0, NG) as g:
                    sp.wait_ge(s["v_ps"], NG * i + g)
                    sp.dma_start(ctxT_g[:, :], ctxT[:, bass.ds(g * GK, GK)]).then_inc(s["ctxT_g_in"], 16)
            sp.wait_ge(s["y_added"], 3 * NG * E8)
            sp.dma_start(out.rearrange("b p d -> p b d"), tiles(x[:, :], NB)).then_inc(s["out_done"], 16)
            sp.wait_ge(s["out_done"], 16)

        @block.gpsimd
        def _(pool):
            pool.memset(ident[:], 0.0).then_inc(s["pool_step"], 1)
            pool.memset(sel[:], 0.0).then_inc(s["pool_step"], 1)
            pool.memset(half[:], -0.5).then_inc(s["pool_step"], 1)
            pool.memset(special[:], 0.0).then_inc(s["pool_step"], 1)
            pool.wait_ge(s["pool_step"], 4)
            pool.affine_select(out=ident[:], in_=ident[:], compare_op=ALU.not_equal, fill=1.0, base=0,
                               pattern=[[-1, P]], channel_multiplier=1).then_inc(s["consts_ready"], 1)
            for r in range(4):
                pool.affine_select(out=special[:], in_=special[:], compare_op=ALU.not_equal, fill=-1.0,
                                   base=-ROW * r - M_ROW, pattern=[[-1, NJ + 1]], channel_multiplier=1).then_inc(s["pool_step"], 1)
                pool.wait_ge(s["pool_step"], 5 + r)
            halves = sel[:, :].rearrange("e (q p) -> e q p", p=P // 2)
            pool.affine_select(out=halves[:, 0:E16, :], in_=halves[:, 0:E16, :], compare_op=ALU.not_equal, fill=1.0,
                               base=0, pattern=[[-1, E16], [0, P // 2]], channel_multiplier=1).then_inc(s["consts_ready"], 1)
            pool.affine_select(out=halves[:, E16:, :], in_=halves[:, E16:, :], compare_op=ALU.not_equal, fill=1.0,
                               base=-E16, pattern=[[0, 2 * CH1 - E16], [0, P // 2]], channel_multiplier=1).then_inc(s["consts_ready"], 1)
            pool.iota(iota_i[:, :], [[1, P]], base=0, channel_multiplier=0).then_inc(s["consts_ready"], 1)

            pool.memset(row_block[:], 1.0).then_inc(s["pool_step"], 1)
            pool.wait_ge(s["pool_step"], 9)
            pool.affine_select(out=row_block[:], in_=row_block[:], compare_op=ALU.is_ge, fill=0.0,
                               base=0, pattern=[[-ROW, 4]], channel_multiplier=1).then_inc(s["pool_step"], 1)
            pool.wait_ge(s["pool_step"], 10)
            pool.affine_select(out=row_block[:], in_=row_block[:], compare_op=ALU.is_ge, fill=0.0,
                               base=ROW - 1, pattern=[[ROW, 4]], channel_multiplier=-1).then_inc(s["pool_step"], 1)
            pool.wait_ge(s["pool_step"], 11)

            def reciprocal_root(n):
                norm = n + 1 if isinstance(n, int) else pool.to_reg(n + 1)
                pool.wait_ge(s["consts_ready"], 4)
                pool.wait_ge(s["ln_var"], norm)
                pool.tensor_scalar(vpe[:], mv[:, :, 1], LN_EPS, None, ALU.add).then_inc(s["ln_vpe"], 1)
                pool.wait_ge(s["ln_vpe"], norm)
                pool.tensor_tensor(rstd[:], vpe[:], half[:], ALU.pow).then_inc(s["ln_rstd"], 1)

            def window(i, g, part):
                if part[0] == "scores":
                    reciprocal_root(attention_norm(i, g))

            def heads(i, g, part):
                a = (i - 1) * NG + g
                if part[0] == "front":
                    reciprocal_root(attention_norm(i, g))
                items = {"queries": (0, 1)}.get(part[0], (part[1] + 2,) if part[0] == "output" and part[1] < GB - 2 else ())
                for b in items:
                    if b < 2:
                        pool.wait_ge(s["k_ready"], a * NJ + NJ)
                    else:
                        pool.wait_ge(s["b_ps"], a * GB + b - 1)
                    kb = ks[:, :, b * KEYS:(b + 1) * KEYS].unsqueeze(2).broadcast_to([P, NJ, 4, KEYS])
                    mask = row_block[:, :].unsqueeze(1).unsqueeze(3).broadcast_to([P, NJ, 4, KEYS])
                    pool.tensor_tensor(kbd[:, b % 2], kb, mask, ALU.mult).then_inc(s["kbd_ready"], 1)

            def experts(i, g, part):
                if part[0] == "front":
                    reciprocal_root(LN_BASE[i] + LN_PER[i] * g)
                elif part[0] == "end" and i == 0:
                    reciprocal_root(LN_BASE[i] + LN_PER[i] * g + 2)

            for _ in steps(pool, window, heads, experts, experts):
                pass

        @block.scalar
        def _(act):
            count = [0]

            def small(dst, src, **kw):
                count[0] += 1
                act.dma_start(dst, src, **kw).then_inc(s["small_in"], 16)

            small(tau[:, :], bc_row(t["condB_tau"], NB))
            small(pt[:, :], bc_row(t["condB_pt"], NB))
            small(lens_i[:, :], bc_row(t["_lenS2"], NB))
            small(r0[:, :], t["L0_ffn_Wg"])
            small(rb0[:, :], bc_row(t["L0_ffn_bg"], E8))
            small(r2[:, :], t["L2_ffn_Wr"])
            small(rb2[:, :], bc_row(t["L2_ffn_br"], E8))
            small(b2_0[:, :], t["L0_ffn_b2"])
            small(b2_2[:, :], t["L2_ffn_b2"])
            small(gamma[:, :], bc_row(t["L0_ffn_gamma"], P))
            small(beta[:, :], bc_row(t["L0_ffn_beta"], P))
            for i in range(3):
                small(bv[i][:, :], bc_row(t[f"L{i + 1}_xcond_bv"], P))
                small(bo[i][:, :], bc_row(t[f"L{i + 1}_xcond_bo"], P))
            act.wait_ge(s["zeroed"], 1)
            for r in range(4):
                for i in range(3):
                    for dst, nm in ((bqs, "bq"), (bks, "bk")):
                        small(dst[i][ROW * r:ROW * r + HD, :],
                              t[f"L{i + 1}_xcond_{nm}"].rearrange("(j r d) -> r d j", j=NJ, r=4)[r], allow_slow_non_contiguous=True)
                small(deltaK[ROW * r + D_ROW:ROW * r + D_ROW + 1, :], t["fside_BxS2_0"].rearrange("(a b) k -> a (b k)", a=1))
            assert count[0] == SMALL_DMAS, count

            def copy_out(dst, src, done):
                act.activation(dst, src, ACT.Copy).then_inc(s[done], 1)

            def window(i, g, part):
                n = g + 1
                if part[0] == "scores":
                    act.wait_ge(s["wa_ps"], n)
                    copy_out(attn[:, 0:GK], psS[:, 0, 0:GK], "wa_ready")
                    act.wait_ge(s["gauss_arg"], n)
                    act.activation(tmp2[:, 0:GK], tmp2[:, 0:GK], ACT.Exp, scale=-1.0 / DEV_POW).then_inc(s["gauss_ready"], 1)
                    act.wait_ge(s["xaT_ps"], n)
                    copy_out(xaT[:, :], psM[:, :], "xaT_ready")
                    act.wait_ge(s["x0_shifted"], n)
                    act.activation(probs[:, 0:GK], probs[:, 0:GK], ACT.Exp).then_inc(s["x0_exp_ready"], 1)
                elif part[0] == "align":
                    act.wait_ge(s["alignT_ps"], n)
                    copy_out(probs[0:KEYS, 1024:1024 + GT], psM[0:KEYS, :], "alignT_ready")
                elif part[0] == "context":
                    act.wait_ge(s["context_ps"], n)
                    copy_out(attnT[:, :], psS[:, 2, :], "context_ready")
                else:
                    act.wait_ge(s["mix_ps"], n)
                    act.activation(tmp[:, :], psS[:, 3, :], ACT.Tanh).then_inc(s["tanh_ready"], 1)

            def heads(i, g, part):
                a = (i - 1) * NG + g
                if part[0] == "front":
                    act.wait_ge(s["xaT_ps"], i * NG + g + 1)
                    copy_out(xaT[:, :], psM[:, :], "xaT_ready")
                elif part[0] == "scores":
                    b = part[1]
                    act.wait_ge(s["b_ps"], a * GB + b + 1)
                    if b:
                        act.wait_ge(s["o_ps"], a * GB + b)
                    act.activation(probs[0:KEYS, :], psS[0:KEYS, :, :].rearrange("p j c -> p (j c)"), ACT.Exp,
                                   scale=SCALE).then_inc(s["probs_ready"], 1)
                elif part[0] == "output":
                    act.wait_ge(s["o_ps"], a * GB + part[1] + 1)
                    copy_out(attnT[:, :], psM[:, :], "oT_ready")
                elif part[0] == "transpose":
                    act.wait_ge(s["attnT_ps"], a + 1)
                    copy_out(attnT[:, :], psM[:, :], "attnT_ready")

            def front(n):
                act.wait_ge(s["xnT_ps"], n + 1)
                copy_out(xnT[:, :], psY[:, :], "xnT_ready")

            def gelu(i, g, e, half):
                m = MOE_OF[i] * NG + g
                for k in (2 * half, 2 * half + 1):
                    c = e * HC + k
                    act.wait_ge(s["h_ps"], m * (E8 * HC) + c + 1)
                    if e >= 2:
                        act.wait_ge(s["y_ps"], m * E8 + e - 1)
                    func = ACT.Relu if i == 2 else ACT.Gelu
                    dst, src = hT[e % 2][:, k, :], psH[:, c % 2, :]
                    if i == 3:
                        act.activation(dst, src, func).then_inc(s["h_ready"], 1)
                    else:
                        b1 = E8 * HC * (i // 2) + c
                        act.activation(dst, src, func, bias=b1T[:, b1:b1 + 1]).then_inc(s["h_ready"], 1)

            def moe(i, g, part):
                f = i * NG + g
                if part[0] == "front":
                    front(f)
                elif part[0] == "route":
                    gelu(i, g, 0, 0)
                    act.wait_ge(s["gap_ready"], f + 1)
                    act.activation(th[:], gap[:], ACT.Tanh, scale=0.5).then_inc(s["gate_ready"], 1)
                    act.wait_ge(s["combT_ps"], f + 1)
                    copy_out(combT[0:E8, :], psY[0:E8, :], "combT_ready")
                elif part[0] == "hidden":
                    gelu(i, g, part[1], part[2])

            def gated(i, g, part):
                f = i * NG + g
                if part[0] == "front":
                    front(f)
                elif part[0] == "route":
                    act.wait_ge(s["gap_ready"], f + 1)
                    act.activation(th[:], gap[:], ACT.Tanh, scale=0.5)
                    act.activation(ths[:], lg[:, :, E16], ACT.Tanh, scale=0.5).then_inc(s["gate_ready"], 1)
                    act.wait_ge(s["combT_ps"], f + 1)
                    copy_out(combT[:, :], psY[0:E16 + 1, :], "combT_ready")
                elif part[0] == "hidden":
                    c = part[1]
                    act.wait_ge(s["f1_ps"], g * CH1 + c + 1)
                    if c >= 2:
                        act.wait_ge(s["f1_h_ready"], g * CH1 + c - 1)
                    act.activation(hT[c % 2][:, 0, :], psH[:, 0, :], ACT.Silu).then_inc(s["silu_ready"], 1)
                elif part[0] == "end":
                    act.wait_ge(s["f1_down"], g * CH1 + CH1)
                    copy_out(hT[0][:, 3, :], psY[:, :], "f1_yT_ready")

            for _ in steps(act, window, heads, moe, gated):
                pass

        @block.vector
        def _(dve):
            chain = {"n": 0, "base": 0, "per": 0, "g": 0}

            def link(ins, alone=False):
                chain["n"] += 1
                ins.then_inc(s["vec_step"], 1)
                value = chain["g"] * chain["per"] + (chain["base"] + chain["n"])
                if alone:
                    value = dve.to_reg(value)
                    dve.wait_ge(s["consts_ready"], 4)
                dve.wait_ge(s["vec_step"], value)

            def memset(buf, v):
                return dve.memset(buf, v)

            for i in range(3):
                memset(bqs[i][:, :], 0.0)
                memset(bks[i][:, :], 0.0)
                memset(wq[i][:, :], 0.0)
                memset(wk[i][:, :], 0.0)
            memset(deltaK[:, :], 0.0).then_inc(s["zeroed"], 1)
            memset(vaug[:, :, :, :], 1.0)
            link(memset(m_pad[:, :], 0.0))
            dve.wait_ge(s["consts_ready"], 4)
            link(dve.tensor_copy(iota[:, :], iota_i[:, :]))
            dve.wait_ge(s["small_in"], 16 * SMALL_DMAS)
            dve.wait_ge(s["pool_step"], 8)
            link(dve.tensor_copy(lens[:, :], lens_i[:, :]))
            dve.tensor_scalar(w_lo[:, :], pt[:, :], -WINDOW, 0.0, ALU.add, ALU.max)
            link(dve.tensor_scalar(w_hi[:, :], pt[:, :], WINDOW, None, ALU.add))
            link(dve.tensor_tensor(w_hi[:, :], w_hi[:, :], lens[:, :], ALU.min))
            for i in range(3):
                for j in range(NJ):
                    dve.tensor_scalar(q_bias[i][:, j, :], tau[:, :], bqs[i][:, j:j + 1], special[:, NJ:NJ + 1], ALU.mult, ALU.subtract)
                last = dve.tensor_tensor(k_bias[i][:, :], bks[i][:, :], special[:, 0:NJ], ALU.add)
            link(last)
            for q in range(PREPS):
                dve.wait_ge(s["prep_ps"], q + 1)
                bank = psS[:, q % 4, :]
                if q < NB // 4:
                    last = dve.tensor_copy(tiles(ctxT[:, q * GK:(q + 1) * GK]), tiles(bank)[:, :, 0:KEYS])
                else:
                    for c in range(4):
                        n = 4 * q + c
                        src = bank[:, c * P:c * P + rows_of[n]]
                        if n == 16:
                            dst = waT[:, :]
                        elif n < 19:
                            dst = wcT[:, n - 17, :]
                        elif n < 31:
                            i, m = divmod(n - 19, 4)
                            dst = (wq[i], wk[i], wvT[i], woT[i])[m][:, :]
                            if m < 2:
                                dst = dst.rearrange("p (h c) -> p h c", c=ROW)[:, :, 0:HD]
                                src = src.rearrange("p (h c) -> p h c", c=HD)
                        elif n < 39:
                            dst = geT[:, (n - 31) * P:(n - 30) * P]
                        elif n < 47:
                            dst = upT[:, (n - 39) * P:(n - 38) * P]
                        elif n < 49:
                            dst = geT[:, (n - 47 + 8) * P:(n - 46 + 8) * P]
                        elif n < 51:
                            dst = upT[:, (n - 49 + 8) * P:(n - 48 + 8) * P]
                        elif n < 61:
                            dst = dnT[:, n - 51, :]
                        else:
                            dst = (r1, r3, b1T)[n - 61][:, :]
                        last = dve.tensor_copy(dst, src)
                last.then_inc(s["prep_sb"], 1)
            dve.wait_ge(s["x_in"], 16)

            def layer_norm(n, src, dst, done=None, scale=None):
                for b in range(GB):
                    last = dve.bn_stats(stats[:, b, :], src(b))
                link(last, alone=True)
                for b in range(GB):
                    last = dve.bn_aggr(mv[:, b, :], stats[:, b, :])
                last.then_inc(s["ln_var"], 1)
                dve.wait_ge(s["ln_rstd"], n + 1)
                r = rstd
                if scale is not None:
                    link(dve.tensor_tensor(rstd_t[:], rstd[:], scale, ALU.mult))
                    r = rstd_t
                for b in range(GB):
                    last = dve.tensor_scalar(tok(dst, b), src(b), mv[:, b, 0:1], r[:, b:b + 1], ALU.subtract, ALU.mult)
                if done:
                    last.then_inc(s[done], 1)
                else:
                    link(last)

            def bcast(small2d, n):
                return small2d.unsqueeze(2).broadcast_to([small2d.shape[0], small2d.shape[1], n])

            def over(ap2d, n):
                return ap2d.unsqueeze(1).broadcast_to([ap2d.shape[0], n, ap2d.shape[1]])

            def window(i, g, part):
                n = g + 1
                keep, gauss, sc, pen = tmp[:, 0:GK], tmp2[:, 0:GK], probs[:, 0:GK], probs[:, 512:512 + GK]
                pos = over(iota[:, 0:KEYS], GB)
                grp = bass.ds(g * GB, GB)
                if part[0] == "scores":
                    layer_norm(attention_norm(i, g), lambda b: x_tile(g, b), xa, done="xa_ready")
                    dve.tensor_tensor(tiles(keep), pos, bcast(w_lo[:, grp], KEYS), ALU.is_ge)
                    link(dve.tensor_tensor(tiles(gauss), pos, bcast(w_hi[:, grp], KEYS), ALU.is_le))
                    link(dve.tensor_tensor(keep, keep, gauss, ALU.mult))
                    link(dve.tensor_tensor(tiles(gauss), pos, bcast(pt[:, grp], KEYS), ALU.subtract))
                    dve.tensor_tensor(gauss, gauss, gauss, ALU.mult).then_inc(s["gauss_arg"], 1)
                    link(dve.tensor_scalar(pen, keep, MASKED, -MASKED, ALU.mult, ALU.add))
                    dve.wait_ge(s["score_ps"], n)
                    link(dve.tensor_tensor(sc, psS[:, 1, 0:GK], keep, ALU.mult))
                    link(dve.tensor_tensor(sc, sc, pen, ALU.add))
                    link(dve.reduce_max(top[:, :], tiles(sc), AX_X))
                    dve.tensor_tensor(tiles(sc), tiles(sc), bcast(top[:, :], KEYS), ALU.subtract).then_inc(s["x0_shifted"], 1)
                    dve.wait_ge(s["x0_exp_ready"], n)
                    link(dve.reduce_sum(den[:, :], tiles(sc), AX_X))
                    link(dve.reciprocal(inv[:, :], den[:, :]))
                    dve.wait_ge(s["gauss_ready"], n)
                    for b in range(GB):
                        last = dve.scalar_tensor_tensor(tiles(sc)[:, b, :], tiles(sc)[:, b, :], inv[:, b:b + 1],
                                                        tiles(gauss)[:, b, :], ALU.mult, ALU.mult)
                    last.then_inc(s["align_ready"], 1)
                elif part[0] == "mix":
                    dve.wait_ge(s["tanh_ready"], n)
                    link(dve.tensor_tensor(x_group(g), x_group(g), tmp[:, :], ALU.add))

            def heads(i, g, part):
                a = (i - 1) * NG + g
                w = i - 1
                grp = bass.ds(g * GB, GB)
                if part[0] == "front":
                    layer_norm(attention_norm(i, g), lambda b: x_tile(g, b), xa, done="xa_ready", scale=tau[:, grp])
                elif part[0] == "keys":
                    for j in range(NJ):
                        dve.wait_ge(s["k_ps"], a * NJ + j + 1)
                        dve.scalar_tensor_tensor(ks[:, j, :], psS[:, j, 0:GK], k_bias[w][:, j:j + 1],
                                                 deltaK[:, bass.ds(g * GK, GK)], ALU.add, ALU.add).then_inc(s["k_ready"], 1)
                elif part[0] == "values":
                    dve.wait_ge(s["v_ps"], a + 1)
                    for b in range(GB):
                        last = dve.tensor_tensor(vaug[:, b, :, 0:HD], psM[0:KEYS, b * P:(b + 1) * P].rearrange("p (h c) -> p h c", c=HD),
                                                 bv[w][0:KEYS, :].rearrange("p (h c) -> p h c", c=HD), ALU.add)
                    last.then_inc(s["v_ready"], 1)
                elif part[0] == "queries":
                    for j in range(NJ):
                        dve.wait_ge(s["q_ps"], a * NJ + j + 1)
                        dve.tensor_tensor(tiles(qs[:, j, :]), tiles(psS[:, j, :]), bcast(q_bias[w][:, j, grp], P),
                                          ALU.add).then_inc(s["q_ready"], 1)
                elif part[0] == "maxima":
                    dve.wait_ge(s["a_ps"], a * GB + part[1] + 1)
                    m_out = m_pad[:, :].rearrange("p (r c) -> p c r", c=ROW)[:, M_ROW:M_ROW + NJ, :]
                    dve.reduce_max(m_out, psS[:, :, 0:GK].rearrange("p j (r k) -> p j r k", k=KEYS), AX_X).then_inc(s["max_ready"], 1)
                elif part[0] == "shift":
                    b = part[1]
                    dve.wait_ge(s["maxT_ps"], a * GB + b + 1)
                    qb = qs[:, :, b * P:(b + 1) * P]
                    dve.tensor_tensor(qb, qb, over(psM[:, 0:P], NJ), ALU.add).then_inc(s["q_shifted"], 1)
                elif part[0] == "divide":
                    b = part[1]
                    dve.wait_ge(s["on_ps"], a * GB + b + 1)
                    ob = psM[:, :].rearrange("p (h c) -> p h c", c=ROW)
                    link(dve.reciprocal(rden[:, b, :], ob[:, :, HD]))
                    dve.tensor_tensor(tok(attn, b).rearrange("p (h c) -> p h c", c=HD), ob[:, :, 0:HD], bcast(rden[:, b, :], HD),
                                      ALU.mult).then_inc(s["attn_ready"], 1)
                elif part[0] == "project":
                    dve.wait_ge(s["wo_ps"], a + 1)
                    dve.tensor_tensor(x_group(g), x_group(g), psS[:, 0, :], ALU.add).then_inc(s["x_done"], 1)
                    dve.wait_ge(s["x_done"], a + 1)
                    link(dve.tensor_tensor(tiles(x_group(g)), tiles(x_group(g)), over(bo[w][:, :], GB), ALU.add))

            def route(f, n_e, width, bias):
                dve.wait_ge(s["logits_ps"], f + 1)
                ps = psY[:, 0:GB * width].rearrange("p (b e) -> p b e", e=width)
                if bias is None:
                    link(dve.tensor_copy(lg[:, :, 0:width], ps), alone=True)
                else:
                    link(dve.tensor_tensor(lg[:, :, 0:width], ps, over(bias[:, :], GB), ALU.add), alone=True)
                for b in range(GB):
                    last = dve.max(mx[:, b, :], lg[:, b, 0:n_e])
                link(last)
                dve.tensor_tensor(gap[:, :], mx[:, :, 0], mx[:, :, 1], ALU.subtract).then_inc(s["gap_ready"], 1)
                for b in range(GB):
                    last = dve.max_index(ix[:, b, :], mx[:, b, :], lg[:, b, 0:n_e])
                link(last)
                link(dve.tensor_copy(ixf[:, :, :], ix[:, :, 0:2]))
                pos = over(iota[:, 0:n_e], GB)
                first, second = oh1[:, :, 0:n_e], oh2[:, :, 0:n_e]
                dve.tensor_tensor(first, pos, bcast(ixf[:, :, 0], n_e), ALU.is_equal)
                dve.tensor_tensor(second, pos, bcast(ixf[:, :, 1], n_e), ALU.is_equal)
                dve.wait_ge(s["gate_ready"], f + 1)
                dve.tensor_scalar(w1[:, :], th[:, :], 0.5, 0.5, ALU.mult, ALU.add)
                link(dve.tensor_scalar(w2[:, :], th[:, :], -0.5, 0.5, ALU.mult, ALU.add))
                dve.tensor_tensor(first, first, bcast(w1[:, :], n_e), ALU.mult)
                link(dve.tensor_tensor(second, second, bcast(w2[:, :], n_e), ALU.mult))
                if width > n_e:
                    dve.tensor_scalar(comb[:, :, n_e], ths[:, :], 0.5, 0.5, ALU.mult, ALU.add)
                dve.tensor_tensor(comb[:, :, 0:n_e], first, second, ALU.add).then_inc(s["comb_ready"], 1)

            def moe(i, g, part):
                f, m = i * NG + g, MOE_OF[i] * NG + g
                acc = (lambda b: tok(xn, b)) if i == 0 else (lambda b: x_tile(g, b))
                acc_all = xn[:, :] if i == 0 else x_group(g)
                ln = LN_BASE[i] + LN_PER[i] * g
                if part[0] == "front":
                    layer_norm(ln, lambda b: x_tile(g, b), xn, done="xn_ready")
                elif part[0] == "route":
                    route(f, E8, E8, {0: rb0, 2: rb2}.get(i))
                    if i < 3:
                        bm = (m if i == 0 else NG + g) + 1
                        dve.wait_ge(s["b2_ps"], bm)
                        dve.tensor_tensor(acc_all, acc_all, psY[:, :], ALU.add).then_inc(s["b2_added"], 1)
                        dve.wait_ge(s["b2_added"], bm)
                elif part[0] == "out":
                    e = part[1]
                    if e:
                        dve.wait_ge(s["y_added"], m * E8 + e)
                    dve.wait_ge(s["y_ps"], m * E8 + e + 1)
                    for b in range(GB):
                        last = dve.scalar_tensor_tensor(acc(b), tok(psY, b), comb[:, b, e:e + 1], acc(b), ALU.mult, ALU.add)
                    last.then_inc(s["y_added"], 1)
                elif part[0] == "end":
                    dve.wait_ge(s["y_added"], m * E8 + E8)
                    if i == 0:
                        layer_norm(ln + 2, lambda b: tok(xn, b), xn)
                        link(dve.tensor_tensor(tiles(xn[:, :]), tiles(xn[:, :]), over(gamma[:, :], GB), ALU.mult))
                        link(dve.tensor_tensor(tiles(xn[:, :]), tiles(xn[:, :]), over(beta[:, :], GB), ALU.add))
                        link(dve.tensor_tensor(x_group(g), x_group(g), xn[:, :], ALU.add))

            def gated(i, g, part):
                if part[0] == "front":
                    layer_norm(LN_BASE[i] + LN_PER[i] * g, lambda b: x_tile(g, b), xn, done="xn_ready")
                elif part[0] == "route":
                    route(NG + g, E16, E16 + 1, None)
                elif part[0] == "weigh":
                    c = part[1]
                    n = g * CH1 + c
                    dve.wait_ge(s["silu_ready"], n + 1)
                    dve.tensor_tensor(hT[c % 2][:, 1, :], hT[c % 2][:, 0, :], psH[:, 1, :], ALU.mult).then_inc(s["f1_t_ready"], 1)
                    dve.wait_ge(s["f1_t_ready"], n + 1)
                    dve.wait_ge(s["f1_w_ps"], n + 1)
                    if c >= 2:
                        dve.wait_ge(s["f1_down"], n - 1)
                    dve.tensor_tensor(hT[c % 2][:, 2, :], hT[c % 2][:, 1, :], psH[:, 0, :], ALU.mult).then_inc(s["f1_h_ready"], 1)
                elif part[0] == "end":
                    dve.wait_ge(s["f1_y_ps"], g + 1)
                    link(dve.tensor_tensor(x_group(g), x_group(g), psH[:, 0, :], ALU.add))

            for what, kind, g in steps(dve, window, heads, moe, gated):
                if what == "end":
                    assert chain["n"] == LINKS[kind], (kind, chain["n"])
                    chain["base"] += (NG - 1) * LINKS[kind]
                    chain["n"], chain["per"], chain["g"] = 0, 0, 0
                else:
                    chain["base"] += chain["n"]
                    chain["n"] = 0
                    if what == "begin":
                        chain["per"], chain["g"] = LINKS[kind], g

        @block.tensor
        def _(pe):
            pe.wait_ge(s["nat_in"], 16 * NAT_DMAS)
            pe.wait_ge(s["consts_ready"], 4)
            for q in range(PREPS):
                if q >= 4:
                    pe.wait_ge(s["prep_sb"], q - 3)
                for c in range(4):
                    n = 4 * q + c
                    rows = rows_of[n]
                    last = pe.transpose(psS[:, q % 4, c * P:c * P + rows], nat[0:rows, n, :], ident[0:rows, 0:rows])
                last.then_inc(s["prep_ps"], 1)
            pe.wait_ge(s["prep_sb"], PREPS)
            pe.wait_ge(s["small_in"], 16 * SMALL_DMAS)

            def mm(o, l, r, start=True, stop=True, **kw):
                return pe.matmul(o, l, r, start=start, stop=stop, **kw)

            def window(i, g, part):
                n = g + 1
                if part[0] == "scores":
                    mm(psS[:, 0, 0:GK], waT[:, :], ctxT[:, bass.ds(g * GK, GK)]).then_inc(s["wa_ps"], 1)
                    pe.wait_ge(s["xa_ready"], n)
                    for b in range(GB):
                        last = pe.transpose(tok(psM, b), tok(xa, b), ident[:, :])
                    last.then_inc(s["xaT_ps"], 1)
                    pe.wait_ge(s["wa_ready"], n)
                    pe.wait_ge(s["xaT_ready"], n)
                    for b in range(GB):
                        last = mm(psS[:, 1, b * KEYS:(b + 1) * KEYS], tok(xaT, b), attn[:, b * KEYS:(b + 1) * KEYS])
                    last.then_inc(s["score_ps"], 1)
                elif part[0] == "align":
                    pe.wait_ge(s["align_ready"], n)
                    for b in range(GB):
                        last = pe.transpose(psM[0:KEYS, b * P:(b + 1) * P], probs[:, b * KEYS:(b + 1) * KEYS], ident[:, :])
                    last.then_inc(s["alignT_ps"], 1)
                elif part[0] == "context":
                    pe.wait_ge(s["alignT_ready"], n)
                    pe.wait_ge(s["ctx_g_in"], n * 16)
                    for b in range(GB):
                        last = mm(psS[:, 2, b * P:(b + 1) * P], ctx_g[:, b, :], probs[0:KEYS, 1024 + b * P:1024 + (b + 1) * P])
                    last.then_inc(s["context_ps"], 1)
                else:
                    pe.wait_ge(s["context_ready"], n)
                    for b in range(GB):
                        mm(psS[:, 3, b * P:(b + 1) * P], tok(attnT, b), wcT[:, 0, :], stop=False)
                        last = mm(psS[:, 3, b * P:(b + 1) * P], tok(xaT, b), wcT[:, 1, :], start=False)
                    last.then_inc(s["mix_ps"], 1)

            def heads(i, g, part):
                w = i - 1
                a = w * NG + g
                if part[0] == "front":
                    pe.wait_ge(s["xa_ready"], i * NG + g + 1)
                    for b in range(GB):
                        last = pe.transpose(tok(psM, b), tok(xa, b), ident[:, :])
                    last.then_inc(s["xaT_ps"], 1)
                elif part[0] == "keys":
                    for j in range(NJ):
                        mm(psS[:, j, 0:GK], wk[w][:, j * P:(j + 1) * P], ctxT[:, bass.ds(g * GK, GK)]).then_inc(s["k_ps"], 1)
                elif part[0] == "values":
                    pe.wait_ge(s["xaT_ready"], i * NG + g + 1)
                    pe.wait_ge(s["ctxT_g_in"], a * 16 + 16)
                    for b in range(GB):
                        last = mm(psM[0:KEYS, b * P:(b + 1) * P], ctxT_g[:, b * KEYS:(b + 1) * KEYS], wvT[w][:, :])
                    last.then_inc(s["v_ps"], 1)
                elif part[0] == "queries":
                    for j in range(NJ):
                        pe.wait_ge(s["k_ready"], a * NJ + j + 1)
                        mm(psS[:, j, :], wq[w][:, j * P:(j + 1) * P], xaT[:, :]).then_inc(s["q_ps"], 1)
                elif part[0] == "maxima":
                    b = part[1]
                    if b:
                        pe.wait_ge(s["probs_ready"], a * GB + b)
                    else:
                        pe.wait_ge(s["q_ready"], a * NJ + NJ)
                        pe.wait_ge(s["v_ready"], a + 1)
                    pe.wait_ge(s["kbd_ready"], a * GB + b + 1)
                    for j in range(NJ):
                        last = mm(psS[:, j, 0:GK], qs[:, j, b * P:(b + 1) * P], kbd[:, b % 2, j].rearrange("p r k -> p (r k)"))
                    last.then_inc(s["a_ps"], 1)
                elif part[0] == "shift":
                    b = part[1]
                    pe.wait_ge(s["max_ready"], a * GB + b + 1)
                    if b:
                        pe.wait_ge(s["attn_ready"], a * GB + b)
                    pe.transpose(psM[:, 0:P], m_pad[:, :], ident[:, :]).then_inc(s["maxT_ps"], 1)
                elif part[0] == "scores":
                    b = part[1]
                    pe.wait_ge(s["q_shifted"], a * GB + b + 1)
                    for j in range(NJ):
                        for r in range(4):
                            last = mm(psS[0:KEYS, j, r * P:(r + 1) * P], kbd[:, b % 2, j, r, :], qs[:, j, b * P:(b + 1) * P])
                    last.then_inc(s["b_ps"], 1)
                elif part[0] == "output":
                    b = part[1]
                    pe.wait_ge(s["probs_ready"], a * GB + b + 1)
                    for h in range(H):
                        j, r = divmod(h, 4)
                        last = mm(psM[ROW * r:ROW * r + HD + 1, j * P:(j + 1) * P], vaug[:, b, h, :], probs[0:KEYS, h * P:(h + 1) * P])
                    last.then_inc(s["o_ps"], 1)
                elif part[0] == "divide":
                    pe.wait_ge(s["oT_ready"], a * GB + part[1] + 1)
                    for j in range(NJ):
                        last = pe.transpose(tok(psM, j), tok(attnT, j), ident[:, :])
                    last.then_inc(s["on_ps"], 1)
                elif part[0] == "transpose":
                    pe.wait_ge(s["attn_ready"], a * GB + GB)
                    for b in range(GB):
                        last = pe.transpose(tok(psM, b), tok(attn, b), ident[:, :])
                    last.then_inc(s["attnT_ps"], 1)
                else:
                    pe.wait_ge(s["attnT_ready"], a + 1)
                    for b in range(GB):
                        last = mm(psS[:, 0, b * P:(b + 1) * P], tok(attnT, b), woT[w][:, :])
                    last.then_inc(s["wo_ps"], 1)

            def front(f, router, width):
                pe.wait_ge(s["xn_ready"], f + 1)
                for b in range(GB):
                    last = pe.transpose(tok(psY, b), tok(xn, b), ident[:, :])
                last.then_inc(s["xnT_ps"], 1)
                pe.wait_ge(s["xnT_ready"], f + 1)
                for b in range(GB):
                    last = mm(psY[:, b * width:(b + 1) * width], tok(xnT, b), router[:, 0:width])
                last.then_inc(s["logits_ps"], 1)

            def comb_transposed(f, width):
                pe.wait_ge(s["comb_ready"], f + 1)
                for b in range(GB):
                    last = pe.transpose(psY[0:width, b * P:(b + 1) * P], comb[:, b, 0:width], ident[:, :])
                last.then_inc(s["combT_ps"], 1)
                pe.wait_ge(s["combT_ready"], f + 1)

            def moe(i, g, part):
                f, m = i * NG + g, MOE_OF[i] * NG + g
                home = moeB if i == 2 else moeA
                router, b2 = {0: (r0, b2_0), 2: (r2, b2_2), 3: (r3, None)}[i]
                wi, wo = w1_of(home), w2_of(home)
                bm = (g if i == 0 else NG + g) + 1

                def hidden(e, half):
                    for k in (2 * half, 2 * half + 1):
                        c = e * HC + k
                        if c >= 2:
                            pe.wait_ge(s["h_ready"], m * (E8 * HC) + c - 1)
                        mm(psH[:, c % 2, :], wi[:, e * HID + k * P:e * HID + (k + 1) * P], xnT[:, :]).then_inc(s["h_ps"], 1)

                if part[0] == "front":
                    front(f, router, E8)
                elif part[0] == "route":
                    hidden(0, 0)
                    comb_transposed(f, E8)
                    if b2 is not None:
                        for b in range(GB):
                            last = mm(tok(psY, b), combT[0:E8, b * P:(b + 1) * P], b2[:, :])
                        last.then_inc(s["b2_ps"], 1)
                elif part[0] == "hidden":
                    hidden(part[1], part[2])
                elif part[0] == "out":
                    e = part[1]
                    pe.wait_ge(s["h_ready"], m * (E8 * HC) + (e + 1) * HC)
                    if e:
                        pe.wait_ge(s["y_added"], m * E8 + e)
                    elif b2 is not None:
                        pe.wait_ge(s["b2_added"], bm)
                    for b in range(GB):
                        for k in range(HC):
                            last = mm(tok(psY, b), hT[e % 2][:, k, b * P:(b + 1) * P], wo[:, e, k, :], start=k == 0, stop=k == HC - 1)
                    last.then_inc(s["y_ps"], 1)

            def gated(i, g, part):
                f = i * NG + g
                if part[0] == "front":
                    front(f, r1, E16 + 1)
                elif part[0] == "route":
                    comb_transposed(f, E16 + 1)
                elif part[0] == "hidden":
                    c = part[1]
                    if c:
                        pe.wait_ge(s["f1_h_ready"], g * CH1 + c)
                    mm(psH[:, 0, :], geT[:, c * P:(c + 1) * P], xnT[:, :])
                    mm(psH[:, 1, :], upT[:, c * P:(c + 1) * P], xnT[:, :]).then_inc(s["f1_ps"], 1)
                elif part[0] == "weigh":
                    c = part[1]
                    pe.wait_ge(s["silu_ready"], g * CH1 + c + 1)
                    mm(psH[:, 0, :], sel[:, c * P:(c + 1) * P], combT[:, :]).then_inc(s["f1_w_ps"], 1)
                elif part[0] == "out":
                    c = part[1]
                    pe.wait_ge(s["f1_h_ready"], g * CH1 + c + 1)
                    mm(psY[:, :], dnT[:, c, :], hT[c % 2][:, 2, :], start=c == 0, stop=c == CH1 - 1).then_inc(s["f1_down"], 1)
                elif part[0] == "end":
                    pe.wait_ge(s["f1_yT_ready"], g + 1)
                    for b in range(GB):
                        last = pe.transpose(psH[:, 0, b * P:(b + 1) * P], hT[0][:, 3, b * P:(b + 1) * P], ident[:, :])
                    last.then_inc(s["f1_y_ps"], 1)

            for what, kind, g in steps(pe, window, heads, moe, gated):
                if what == "load":
                    home, times = {0: ("moeA_in", 1), 2: ("moeB_in", 1), 3: ("moeA_in", 2)}[g]
                    pe.wait_ge(s[home], times * 16 * MOE_DMAS)


def kernel(**inputs):
    import numpy as _np
    import concourse.bacc as _bacc
    from concourse import mybir as _mybir
    from concourse.bass_utils import run_bass_kernel_spmd as _run

    nc = _bacc.Bacc("TRN2", target_bir_lowering=False, num_devices=1)
    arrays, t = {}, {}
    for name, value in inputs.items():
        a = _np.ascontiguousarray(value)
        arrays[f"in_{name}"] = a
        t[name] = nc.dram_tensor(f"in_{name}", a.shape, _mybir.dt.from_np(a.dtype), kind="ExternalInput").ap()
    out = nc.dram_tensor("out_x", inputs["x"].shape, _mybir.dt.float32, kind="ExternalOutput").ap()
    build(nc, t, out)
    r = _run(nc, [arrays], core_ids=[0])
    return r.results[0]["out_x"]
```

```python
from contextlib import ExitStack

import concourse.bass as bass
from concourse import mybir

F32 = mybir.dt.float32
F32R = mybir.dt.float32r
I32 = mybir.dt.int32
U32 = mybir.dt.uint32
ALU = mybir.AluOpType
ACT = mybir.ActivationFunctionType
AX_X = mybir.AxisListType.X

P = 128
NB = 16
GB = 4
NG = NB // GB
GT = GB * P
KEYS = 120
GK = GB * KEYS
H, HD = 16, 8
ROW = 32
NJ = 4
M_ROW = 24
D_ROW = 28
HI_MASK = -4096
E8, HID, HC = 8, 512, 4
E16, CH1 = 16, 10
LN_EPS = 1e-5
WINDOW, DEV_POW = 16.0, 128.0
MASKED = 1.0e9
SCALE = float(HD) ** -0.5

LINKS = {"f0x0": 23, "f0x1": 0, "f1x1": 23, "f1x2": 0, "f2x2": 22, "f2x3": 0, "f3x3": 22, "f3": 0}

LN_BASE, LN_PER = [2, 3 * NG + 2, 5 * NG + 2, 7 * NG + 2], [3, 2, 2, 2]
MOE_OF = {0: 0, 2: 1, 3: 2}


COST = {"hidden": 1, "out": 4, "up": 1, "swish": 1, "weigh": 1}
GATED_COST = {**COST, "out": 1}
FILL = {"values": 1, "queries": 1, "maxima": 4, "shift": 1, "scores": 1, "divide": 1, "wait_exp": 4, "transpose": 1, "project": 1,
        "align": 11, "context": 1, "mix": 1}
FIRST = {"maxima": 6, "shift": 3}
GATED_FILL = {**FILL, "front": 1, "keys_read": 1, "maxima": 2, "wait_exp": 2}
GATED_FIRST = {"maxima": 1, "shift": 2}


def merged(experts, attention, cost, fill, first):
    order, left = [], list(experts)

    def take():
        part = left.pop(0)
        order.append(("ahead", part[1:]) if part[0] == "ahead" else ("experts", part))
        return cost.get(part[0], 0)

    for part in attention:
        need, got = fill.get(part[0], 0), 0
        if part[0] in first and part[1] == 0:
            need = first[part[0]]
        while left and left[0] != ("ahead", "norm") and got < need:
            got += take()
        order.append(("attention", part))
    while left:
        take()
    return order


WINDOW_PARTS = [("norm",), ("scores",), ("align",), ("context",), ("mix",)]
HEADS_PARTS = ([("norm",), ("keys",), ("front",)] + [("keys_read", _j) for _j in range(NJ)] + [("values",)]
               + [("queries", _j) for _j in range(NJ)] + [("maxima", 0), ("shift", 0), ("scores", 0)])
for _b in range(GB):
    if _b + 1 < GB:
        HEADS_PARTS += [("maxima", _b + 1), ("output", _b), ("divide", _b), ("shift", _b + 1), ("scores", _b + 1)]
    else:
        HEADS_PARTS += [("wait_exp", _b), ("output", _b), ("divide", _b)]
HEADS_PARTS += [("transpose",), ("project",)]


def moe_parts(gate_at, comb_at, b2_at):
    chunks = [("hidden", e, k) for e in range(E8) for k in range(HC)]
    parts = [("logits",)]
    for c, chunk in enumerate(chunks):
        parts += [("gate",)] * (c == gate_at) + [("comb",)] * (c == comb_at) + [("b2",)] * (c == b2_at)
        parts += [("ahead", "norm")] * (c == E8 * HC - 2) + [chunk]
        if c >= 2 * HC - 1 and c % HC == HC - 1:
            parts += [("out", c // HC - 1)]
    return parts + [("ahead", "front"), ("out", E8 - 1), ("end",)]


MOE_PARTS = {0: moe_parts(4, 6, 7), 2: moe_parts(2, 6, 7), 3: moe_parts(2, 6, 7)}
GATED_PARTS = [("logits",), ("up", 0), ("swish", 0), ("gate",), ("comb",), ("weigh", 0)]
for _c in range(1, CH1):
    GATED_PARTS += [("up", _c), ("swish", _c), ("out", _c - 1), ("weigh", _c)]
GATED_PARTS += [("out", CH1 - 1), ("ahead", "front"), ("end",)]
GATED_PARTS.insert(GATED_PARTS.index(("up", CH1 - 1)), ("ahead", "norm"))


def schedule(layer, group_is_last):
    experts = GATED_PARTS if layer == 1 else MOE_PARTS[layer]
    if layer == 3 and group_is_last:
        return [("experts", p) for p in experts if p[0] != "ahead"]
    attention = WINDOW_PARTS if layer == 0 and not group_is_last else HEADS_PARTS
    early = [p for p in attention if p[0] in ("norm", "keys")]
    gate, comb = experts.index(("gate",)) + 1, experts.index(("b2",) if attention is WINDOW_PARTS else ("comb",)) + 1
    return ([("experts", p) for p in experts[:gate]] + [("attention", p) for p in early] + [("experts", p) for p in experts[gate:comb]]
            + merged(experts[comb:], attention[len(early):], *((GATED_COST, GATED_FILL, GATED_FIRST) if layer == 1 else (COST, FILL, FIRST))))


def pair_rows(w):
    return w.rearrange("e h d -> (e h) d").rearrange("(c a) d -> a c d", a=P)


def build(nc, t, out):
    ctx = ExitStack()
    with ctx:
        def sb(name, shape, dt=F32):
            return ctx.enter_context(nc.sbuf_tensor(name, shape, dt))

        def sem(name):
            return ctx.enter_context(nc.semaphore(name))

        x = sb("x", [P, NB * P])
        xa = sb("xa", [P, GT])
        xaT = sb("xaT", [P, GT])
        xnT = sb("xnT", [P, GT])
        xn = sb("xn", [P, GT])
        ctxT = sb("ctxT", [P, NB * KEYS])
        ctxT_g = sb("ctxT_g", [P, GK])
        ident = sb("ident", [P, P])
        wq = [sb(f"wq{i}", [P, H * ROW]) for i in range(3)]
        wk = [sb(f"wk{i}", [P, H * ROW]) for i in range(3)]
        wvT = [sb(f"wvT{i}", [P, P]) for i in range(3)]
        woT = [sb(f"woT{i}", [P, P]) for i in range(3)]
        bv = [sb(f"bv{i}", [P, P]) for i in range(3)]
        bo = [sb(f"bo{i}", [P, P]) for i in range(3)]
        bqk = sb("bqk", [P, 6, NJ])
        q_bias = [sb(f"q_bias{i}", [P, NJ, NB]) for i in range(3)]
        k_bias = [sb(f"k_bias{i}", [P, NJ]) for i in range(3)]
        row_of = sb("row_of", [P, ROW])
        q_is_lo = sb("q_is_lo", [P, 1])
        k_is_lo = sb("k_is_lo", [P, 1])
        k_sign = sb("k_sign", [P, 1])
        q_special = sb("q_special", [P, 1])
        deltaK = sb("deltaK", [P, NB * KEYS])
        waT = sb("waT", [P, P])
        wcT = sb("wcT", [P, 2, P])
        moeA = sb("moeA", [P, 2 * E8 * HID])
        moeB = sb("moeB", [P, 2 * E8 * HID])
        nat = moeB[:, :].rearrange("p (s c) -> p s c", c=P)
        geT = sb("geT", [P, CH1 * P])
        upT = sb("upT", [P, CH1 * P])
        dnT = sb("dnT", [P, CH1, P])
        r0 = sb("r0", [P, E8])
        r1 = sb("r1", [P, E16 + 1])
        r2 = sb("r2", [P, E8])
        r3 = sb("r3", [P, E8])
        rb0 = sb("rb0", [P, E8])
        rb2 = sb("rb2", [P, E8])
        b1T = sb("b1T", [P, 2 * E8 * HC])
        b2_0 = sb("b2_0", [E8, P])
        b2_2 = sb("b2_2", [E8, P])
        gamma = sb("gamma", [P, P])
        beta = sb("beta", [P, P])
        tau = sb("tau", [P, NB])
        pt = sb("pt", [P, NB])
        lens_i = sb("lens_i", [P, NB], I32)
        lens = sb("lens", [P, NB])
        w_lo = sb("w_lo", [P, NB])
        w_hi = sb("w_hi", [P, NB])
        iota_i = sb("iota_i", [P, P], I32)
        iota = sb("iota", [P, P])
        half = sb("half", [P, GB])
        sel = sb("sel", [E16 + 1, CH1 * P])
        stats = sb("stats", [P, GB, 6])
        mv = sb("mv", [P, GB, 2])
        vpe = sb("vpe", [P, GB])
        rstd = sb("rstd", [P, GB])
        rstd_t = sb("rstd_t", [P, GB])
        qs = sb("qs", [P, NJ, GT], F32R)
        ks = sb("ks", [P, NJ, GK])
        vaug = sb("vaug", [KEYS, GB, H, HD + 1])
        probs = sb("probs", [P, 4 * 512])
        xw = probs[:, 3 * 512:]
        m_pad = sb("m_pad", [P, P])
        rden = sb("rden", [P, GB, H])
        top = sb("top", [P, GB])
        den = sb("den", [P, GB])
        inv = sb("inv", [P, GB])
        attn = sb("attn", [P, GT])
        attnT = sb("attnT", [P, GT])
        q_shift = attnT[:, :]
        row_block = sb("row_block", [P, 4])
        lg = sb("lg", [P, GB, E16 + 1])
        mx = sb("mx", [P, GB, 8])
        ix = sb("ix", [P, GB, 8], U32)
        ixf = sb("ixf", [P, GB, 2])
        oh1 = sb("oh1", [P, GB, E16])
        oh2 = sb("oh2", [P, GB, E16])
        gap = sb("gap", [P, GB])
        th = sb("th", [P, GB])
        ths = sb("ths", [P, GB])
        w1 = sb("w1", [P, GB])
        w2 = sb("w2", [P, GB])
        comb = sb("comb", [P, GB, E16 + 1])
        combT = sb("combT", [E16 + 1, GT])
        hT = [sb(f"hT{i}", [P, HC, GT]) for i in range(2)]

        with nc.sbuf_tensor("kbd", [P, 2, NJ, 4, KEYS], F32R) as kbd:
            pass
        tmp = sb("tmp", [P, GT])
        tmp2 = sb("tmp2", [P, GT])
        ctx_g = sb("ctx_g", [KEYS, GB, P])
        sb("kbd_rest", [P, 2 * NJ * 4 * KEYS - 3 * GT])

        psS = ctx.enter_context(nc.psum_tensor("psS", [P, 4, 512], F32))
        psH = ctx.enter_context(nc.psum_tensor("psH", [P, 2, 512], F32))
        psY = ctx.enter_context(nc.psum_tensor("psY", [P, 512], F32))
        psM = ctx.enter_context(nc.psum_tensor("psM", [P, 512], F32))

        names = """cond_in x_in ctx_in window_in nat_in head_bias_in head_bias_ready small_in moeA_in moeB_in ctx_g_in ctxT_g_in out_done
            zeroed consts_ready pool_step prep_ps prep_sb vec_step
            ln_var ln_vpe ln_rstd xn_ready xnT_ps xnT_ready xa_ready xaT_ps xaT_ready
            wa_ps wa_ready score_ps gauss_arg gauss_ready x0_shifted x0_exp_ready align_ready alignT_ps alignT_ready
            context_ps context_ready mix_ps tanh_ready x0_done
            k_ps k_read k_ready kbd_ready v_ps v_ready q_ps q_read q_ready a_ps max_ready maxT_ps q_shifted b_ps probs_ready o_ps oT_ready on_ps attn_ready
            attnT_ps attnT_ready wo_ps x_done
            logits_ps gap_ready gate_ready comb_ready combT_ps combT_ready b2_ps b2_added
            h_ps h_ready y_ps y_added f0_done
            f1_ps f1_up_ps silu_ready f1_t_ready f1_w_ps f1_h_ready f1_down f1_yT_ready f1_y_ps""".split()
        s = {n: sem(n) for n in names}

        def bc_row(row, n):
            return row.rearrange("(a n) -> a n", a=1).broadcast_to([P, n])

        def tok(buf, b=0, n=1):
            return buf[:, b * P:(b + n) * P]

        def tiles(ap2d, n=GB):
            return ap2d.rearrange("p (b c) -> p b c", b=n)

        def x_tile(g, b):
            return x[:, bass.ds(g * GT + b * P, P)]

        def x_group(g):
            return x[:, bass.ds(g * GT, GT)]

        def w1_of(home):
            return home[:, 0:E8 * HID]

        def w2_of(home):
            return home[:, E8 * HID:].rearrange("p (e k d) -> p e k d", e=E8, k=HC)

        SLOTS = 64
        head_bias = nat[0:6 * NJ, 62, :].rearrange("n (r c) -> n r c", c=ROW)
        rows_of = [KEYS] * NB + [P] * (SLOTS - NB)
        rows_of[61], rows_of[62], rows_of[63] = E16 + 1 + E8, 6 * NJ, 2 * E8 * HC
        CTX_DMAS, WINDOW_DMAS, NAT_DMAS, COND_DMAS, SMALL_DMAS, MOE_DMAS = 1, 3, 22, 3, 14 + 4, 1 + E8
        PREPS = SLOTS // 4
        PREP_ORDER = [range(0, 5), (), range(5, 12), range(12, 14), range(14, PREPS)]

        def prep_bank(q):
            return psS[:, q % 4, :] if q < 5 else psH[:, (q - 5) % 3, :] if (q - 5) % 3 < 2 else psY[:, :]

        def prep_before(q):
            return {4: 1}.get(q, max(0, q - 2) if q >= 8 else 0)

        def attention_norm(i, g):
            if isinstance(g, int):
                return LN_BASE[i - 1] + LN_PER[i - 1] * (NG - 1) if i else 0
            return LN_BASE[i] + LN_PER[i] * (g - 1)

        def experts_norm(i, g):
            return attention_norm(i, g) + 1

        def steps(eng, window, heads, moe, gated, ahead):
            for slots, part in zip(PREP_ORDER, WINDOW_PARTS):
                for q in slots:
                    yield ("prep", None, q)
                if part == ("norm",):
                    yield ("window_tables", None, None)
                window(0, 0, part)
            ahead(0, 0, ("norm",))
            yield ("tables", None, None)
            ahead(0, 0, ("front",))
            for i in range(4):
                experts, beside = (gated if i == 1 else moe), (window if i == 0 else heads)
                if i != 1:
                    yield ("load", None, i)
                with eng.Fori(0, NG - 1) as g:
                    yield ("begin", f"f{i}x{i}", g)
                    for who, part in schedule(i, False):
                        if who == "experts":
                            experts(i, g, part)
                        elif who == "ahead":
                            ahead(i, g + 1, part)
                        else:
                            beside(i, g + 1, part)
                    yield ("end", f"f{i}x{i}", g)
                yield ("once", None, None)
                for who, part in schedule(i, True):
                    if who == "experts":
                        experts(i, NG - 1, part)
                    elif who == "ahead":
                        ahead(i + 1, 0, part)
                    else:
                        heads(i + 1, 0, part)

        block = ctx.enter_context(nc.Block())

        @block.sync
        def _(sp):
            count = [0]

            def nat_load(dst, src):
                count[0] += 1
                done = "ctx_in" if count[0] <= CTX_DMAS else "window_in" if count[0] <= CTX_DMAS + WINDOW_DMAS else "nat_in"
                sp.dma_start(dst, src).then_inc(s[done], 16)

            def moe_load(home, w1d, w2d, done):
                sp.dma_start(w1_of(home).rearrange("p (e h) -> p e h", e=E8), w1d.rearrange("e d h -> d e h")).then_inc(done, 16)
                for e in range(E8):
                    sp.dma_start(w2_of(home)[:, e], w2d[e].rearrange("(k p) d -> p k d", k=HC)).then_inc(done, 16)

            nat_load(nat[0:KEYS, 0:NB, :], t["ctx_1024"].rearrange("b k d -> k b d"))
            nat_load(nat[:, 16, :], t["L0_xcond_W_a"])
            nat_load(nat[:, 17:19, :], t["L0_xcond_W_c"].rearrange("o (h k) -> o h k", h=2))
            nat_load(nat[:, 19, :], t["L1_xcond_Wq"])
            sp.dma_start(tiles(x[:, :], NB), t["x"].rearrange("b p d -> p b d")).then_inc(s["x_in"], 16)
            sp.dma_start(ctx_g[:, :, :], t["ctx_1024"][0:GB].rearrange("b k d -> k b d")).then_inc(s["ctx_g_in"], 16)
            for i in range(3):
                for m, w in enumerate("qkvo"):
                    if i == 0 and m == 0:
                        continue
                    nat_load(nat[:, 19 + 4 * i + m, :], t[f"L{i + 1}_xcond_W{w}"])
            nat_load(nat[:, 31:39, :], pair_rows(t["L1_ffn_We_gate"]))
            nat_load(nat[:, 39:47, :], pair_rows(t["L1_ffn_We_up"]))
            nat_load(nat[:, 47:49, :], t["L1_ffn_Ws_gate"].rearrange("(c h) d -> h c d", c=2))
            nat_load(nat[:, 49:51, :], t["L1_ffn_Ws_up"].rearrange("(c h) d -> h c d", c=2))
            nat_load(nat[:, 51:59, :].rearrange("p c (a h) -> p (c a) h", a=2), t["L1_ffn_We_down"].rearrange("e d h -> d e h"))
            nat_load(nat[:, 59:61, :], t["L1_ffn_Ws_down"].rearrange("d (c h) -> d c h", c=2))
            nat_load(nat[0:E16, 61, :], t["L1_ffn_Wg"])
            nat_load(nat[E16:E16 + 1, 61, :], t["L1_ffn_Wsg"])
            nat_load(nat[E16 + 1:E16 + 1 + E8, 61, :], t["L3_ffn_router_w"])
            nat_load(nat[0:32, 63, :], t["L0_ffn_b1"].rearrange("e (k p) -> (e k) p", k=HC))
            nat_load(nat[32:64, 63, :], t["L2_ffn_b1"].rearrange("e (k p) -> (e k) p", k=HC))
            assert count[0] == CTX_DMAS + WINDOW_DMAS + NAT_DMAS, count
            moe_load(moeA, t["L0_ffn_W1"], t["L0_ffn_W2"], s["moeA_in"])
            with sp.Fori(1, NG) as g:
                sp.wait_ge(s["context_ps"], g)
                sp.dma_start(ctx_g[:, :, :], t["ctx_1024"][bass.ds(g * GB, GB)].rearrange("b k d -> k b d")).then_inc(s["ctx_g_in"], 16)
            sp.wait_ge(s["prep_ps"], PREPS)
            moe_load(moeB, t["L2_ffn_W1"], t["L2_ffn_W2"], s["moeB_in"])
            sp.wait_ge(s["prep_sb"], PREPS)
            for i in range(3):
                if i == 0:
                    sp.dma_start(ctxT_g[:, :], ctxT[:, 0:GK]).then_inc(s["ctxT_g_in"], 16)
                    sp.wait_ge(s["y_added"], NG * E8)
                    moe_load(moeA, t["L3_ffn_w1"], t["L3_ffn_w2"], s["moeA_in"])
                with sp.Fori(1 if i == 0 else 0, NG) as g:
                    sp.wait_ge(s["v_ps"], NG * i + g)
                    sp.dma_start(ctxT_g[:, :], ctxT[:, bass.ds(g * GK, GK)]).then_inc(s["ctxT_g_in"], 16)
            sp.wait_ge(s["y_added"], 3 * NG * E8)
            sp.dma_start(out.rearrange("b p d -> p b d"), tiles(x[:, :], NB)).then_inc(s["out_done"], 16)
            sp.wait_ge(s["out_done"], 16)

        @block.gpsimd
        def _(pool):
            pool.memset(ident[:], 0.0).then_inc(s["pool_step"], 1)
            pool.memset(sel[:], 0.0).then_inc(s["pool_step"], 1)
            pool.memset(half[:], -0.5).then_inc(s["pool_step"], 1)
            pool.memset(row_of[:], 0.0).then_inc(s["pool_step"], 1)
            pool.wait_ge(s["pool_step"], 4)
            pool.affine_select(out=ident[:], in_=ident[:], compare_op=ALU.not_equal, fill=1.0, base=0,
                               pattern=[[-1, P]], channel_multiplier=1).then_inc(s["consts_ready"], 1)
            for r in range(4):
                pool.affine_select(out=row_of[:], in_=row_of[:], compare_op=ALU.not_equal, fill=1.0,
                                   base=-ROW * r, pattern=[[-1, ROW]], channel_multiplier=1).then_inc(s["pool_step"], 1)
                pool.wait_ge(s["pool_step"], 5 + r)
            halves = sel[:, :].rearrange("e (q p) -> e q p", p=P // 2)
            pool.affine_select(out=halves[:, 0:E16, :], in_=halves[:, 0:E16, :], compare_op=ALU.not_equal, fill=1.0,
                               base=0, pattern=[[-1, E16], [0, P // 2]], channel_multiplier=1).then_inc(s["consts_ready"], 1)
            pool.affine_select(out=halves[:, E16:, :], in_=halves[:, E16:, :], compare_op=ALU.not_equal, fill=1.0,
                               base=-E16, pattern=[[0, 2 * CH1 - E16], [0, P // 2]], channel_multiplier=1).then_inc(s["consts_ready"], 1)
            pool.iota(iota_i[:, :], [[1, P]], base=0, channel_multiplier=0).then_inc(s["consts_ready"], 1)

            pool.memset(row_block[:], 1.0).then_inc(s["pool_step"], 1)
            pool.wait_ge(s["pool_step"], 9)
            pool.affine_select(out=row_block[:], in_=row_block[:], compare_op=ALU.is_ge, fill=0.0,
                               base=0, pattern=[[-ROW, 4]], channel_multiplier=1).then_inc(s["pool_step"], 1)
            pool.wait_ge(s["pool_step"], 10)
            pool.affine_select(out=row_block[:], in_=row_block[:], compare_op=ALU.is_ge, fill=0.0,
                               base=ROW - 1, pattern=[[ROW, 4]], channel_multiplier=-1).then_inc(s["pool_step"], 1)
            pool.wait_ge(s["pool_step"], 11)

            def reciprocal_root(n):
                norm = n + 1 if isinstance(n, int) else pool.to_reg(n + 1)
                pool.wait_ge(s["consts_ready"], 4)
                pool.wait_ge(s["ln_var"], norm)
                pool.tensor_scalar(vpe[:], mv[:, :, 1], LN_EPS, None, ALU.add).then_inc(s["ln_vpe"], 1)
                pool.wait_ge(s["ln_vpe"], norm)
                pool.tensor_tensor(rstd[:], vpe[:], half[:], ALU.pow).then_inc(s["ln_rstd"], 1)

            def window(i, g, part):
                if part[0] == "norm":
                    reciprocal_root(attention_norm(i, g))

            def heads(i, g, part):
                a = (i - 1) * NG + g
                if part[0] == "norm":
                    reciprocal_root(attention_norm(i, g))
                items = (0, 1) if part == ("queries", 0) else (part[1] + 2,) if part[0] == "output" and part[1] < GB - 2 else ()
                for b in items:
                    if b < 2:
                        pool.wait_ge(s["k_ready"], a * NJ + NJ)
                    else:
                        pool.wait_ge(s["b_ps"], a * GB + b - 1)
                    kb = ks[:, :, b * KEYS:(b + 1) * KEYS].unsqueeze(2).broadcast_to([P, NJ, 4, KEYS])
                    mask = row_block[:, :].unsqueeze(1).unsqueeze(3).broadcast_to([P, NJ, 4, KEYS])
                    pool.tensor_tensor(kbd[:, b % 2], kb, mask, ALU.mult).then_inc(s["kbd_ready"], 1)

            def experts(i, g, part):
                if part[0] == "end" and i == 0:
                    reciprocal_root(LN_BASE[i] + LN_PER[i] * g + 2)

            def ahead(i, g, part):
                if part[0] == "norm":
                    reciprocal_root(experts_norm(i, g))

            for _ in steps(pool, window, heads, experts, experts, ahead):
                pass

        @block.scalar
        def _(act):
            count = [0]

            def small(dst, src, **kw):
                count[0] += 1
                act.dma_start(dst, src, **kw).then_inc(s["small_in"], 16)

            for dst, nm in ((tau, "condB_tau"), (pt, "condB_pt"), (lens_i, "_lenS2")):
                act.dma_start(dst[:, :], bc_row(t[nm], NB)).then_inc(s["cond_in"], 16)
            def small_loads():
                act.wait_ge(s["zeroed"], 1)
                for i in range(3):
                    for m, nm in enumerate(("bq", "bk")):
                        n = 2 * NJ * i + NJ * m
                        act.dma_start(head_bias[n:n + NJ, :, 0:HD], t[f"L{i + 1}_xcond_{nm}"].rearrange("(j r d) -> j r d", j=NJ, r=4)
                                      ).then_inc(s["head_bias_in"], 16)
                small(r0[:, :], t["L0_ffn_Wg"])
                small(rb0[:, :], bc_row(t["L0_ffn_bg"], E8))
                small(r2[:, :], t["L2_ffn_Wr"])
                small(rb2[:, :], bc_row(t["L2_ffn_br"], E8))
                small(b2_0[:, :], t["L0_ffn_b2"])
                small(b2_2[:, :], t["L2_ffn_b2"])
                small(gamma[:, :], bc_row(t["L0_ffn_gamma"], P))
                small(beta[:, :], bc_row(t["L0_ffn_beta"], P))
                for i in range(3):
                    small(bv[i][:, :], bc_row(t[f"L{i + 1}_xcond_bv"], P))
                    small(bo[i][:, :], bc_row(t[f"L{i + 1}_xcond_bo"], P))
                for r in range(4):
                    small(deltaK[ROW * r + D_ROW:ROW * r + D_ROW + 2, :],
                          t["fside_BxS2_0"].rearrange("(a b) k -> a (b k)", a=1).broadcast_to([2, NB * KEYS]))
                assert count[0] == SMALL_DMAS, count

            def copy_out(dst, src, done):
                act.activation(dst, src, ACT.Copy).then_inc(s[done], 1)

            def window(i, g, part):
                n = g + 1
                if part[0] == "scores":
                    act.wait_ge(s["wa_ps"], n)
                    copy_out(attn[:, 0:GK], psS[:, 0, 0:GK], "wa_ready")
                    act.wait_ge(s["xaT_ps"], n)
                    copy_out(xaT[:, :], psM[:, :], "xaT_ready")
                    act.wait_ge(s["gauss_arg"], n)
                    act.activation(tmp2[:, 0:GK], tmp2[:, 0:GK], ACT.Exp, scale=-1.0 / DEV_POW).then_inc(s["gauss_ready"], 1)
                    act.wait_ge(s["x0_shifted"], n)
                    act.activation(probs[:, 0:GK], probs[:, 0:GK], ACT.Exp).then_inc(s["x0_exp_ready"], 1)
                elif part[0] == "align":
                    act.wait_ge(s["alignT_ps"], n)
                    copy_out(probs[0:KEYS, 1024:1024 + GT], psM[0:KEYS, :], "alignT_ready")
                elif part[0] == "context":
                    act.wait_ge(s["context_ps"], n)
                    copy_out(attnT[:, :], psS[:, 2, :], "context_ready")
                elif part[0] == "mix":
                    act.wait_ge(s["mix_ps"], n)
                    act.activation(tmp[:, :], psS[:, 3, :], ACT.Tanh).then_inc(s["tanh_ready"], 1)

            def heads(i, g, part):
                a = (i - 1) * NG + g
                if part[0] == "front":
                    act.wait_ge(s["xaT_ps"], i * NG + g + 1)
                    copy_out(xaT[:, :], psM[:, :], "xaT_ready")
                elif part[0] == "scores":
                    b = part[1]
                    act.wait_ge(s["b_ps"], a * GB + b + 1)
                    if b:
                        act.wait_ge(s["o_ps"], a * GB + b)
                    act.activation(probs[0:KEYS, :], psS[0:KEYS, :, :].rearrange("p j c -> p (j c)"), ACT.Exp,
                                   scale=SCALE).then_inc(s["probs_ready"], 1)
                elif part[0] == "output":
                    act.wait_ge(s["o_ps"], a * GB + part[1] + 1)
                    copy_out(attnT[:, :], psM[:, :], "oT_ready")
                elif part[0] == "transpose":
                    act.wait_ge(s["attnT_ps"], a + 1)
                    copy_out(attnT[:, :], psM[:, :], "attnT_ready")

            def ahead(i, g, part):
                if part[0] == "front":
                    act.wait_ge(s["xnT_ps"], i * NG + g + 1)
                    copy_out(xnT[:, :], psM[:, :], "xnT_ready")

            def gelu(i, g, e, k):
                m = MOE_OF[i] * NG + g
                c = e * HC + k
                act.wait_ge(s["h_ps"], m * (E8 * HC) + c + 1)
                if e >= 2:
                    act.wait_ge(s["y_ps"], m * E8 + e - 1)
                func = ACT.Relu if i == 2 else ACT.Gelu
                dst, src = hT[e % 2][:, k, :], psH[:, c % 2, :]
                if i == 3:
                    act.activation(dst, src, func).then_inc(s["h_ready"], 1)
                else:
                    b1 = E8 * HC * (i // 2) + c
                    act.activation(dst, src, func, bias=b1T[:, b1:b1 + 1]).then_inc(s["h_ready"], 1)

            def moe(i, g, part):
                f = i * NG + g
                if part[0] == "gate":
                    act.wait_ge(s["gap_ready"], f + 1)
                    act.activation(th[:], gap[:], ACT.Tanh, scale=0.5).then_inc(s["gate_ready"], 1)
                elif part[0] == "comb" and i < 3:
                    act.wait_ge(s["combT_ps"], f + 1)
                    copy_out(combT[0:E8, :], psY[0:E8, :], "combT_ready")
                elif part[0] == "hidden":
                    gelu(i, g, part[1], part[2])

            def gated(i, g, part):
                f = i * NG + g
                if part[0] == "gate":
                    act.wait_ge(s["gap_ready"], f + 1)
                    act.activation(th[:], gap[:], ACT.Tanh, scale=0.5)
                    act.activation(ths[:], lg[:, :, E16], ACT.Tanh, scale=0.5).then_inc(s["gate_ready"], 1)
                elif part[0] == "comb":
                    act.wait_ge(s["combT_ps"], f + 1)
                    copy_out(combT[:, :], psY[0:E16 + 1, :], "combT_ready")
                elif part[0] == "swish":
                    c = part[1]
                    act.wait_ge(s["f1_ps"], g * CH1 + c + 1)
                    if c >= 2:
                        act.wait_ge(s["f1_h_ready"], g * CH1 + c - 1)
                    act.activation(hT[c % 2][:, 0, :], psH[:, 0, :], ACT.Silu).then_inc(s["silu_ready"], 1)
                elif part[0] == "end":
                    act.wait_ge(s["f1_down"], g * CH1 + CH1)
                    copy_out(hT[0][:, 3, :], psY[:, :], "f1_yT_ready")

            for what, _, q in steps(act, window, heads, moe, gated, ahead):
                if (what, q) == ("prep", NB // 4 + 1):
                    small_loads()

        @block.vector
        def _(dve):
            chain = {"n": 0, "base": 0, "per": 0, "g": 0}

            def wait_alone(semaphore, value):
                value = dve.to_reg(value)
                dve.wait_ge(s["consts_ready"], 4)
                dve.wait_ge(semaphore, value)

            def link(ins, alone=False):
                chain["n"] += 1
                ins.then_inc(s["vec_step"], 1)
                value = chain["g"] * chain["per"] + (chain["base"] + chain["n"])
                if alone:
                    wait_alone(s["vec_step"], value)
                else:
                    dve.wait_ge(s["vec_step"], value)

            def memset(buf, v):
                return dve.memset(buf, v)

            memset(head_bias[:, :, :], 0.0)
            memset(deltaK[:, :], 0.0).then_inc(s["zeroed"], 1)
            for i in range(3):
                memset(wq[i][:, :], 0.0)
                memset(wk[i][:, :], 0.0)
            
            memset(vaug[:, :, :, :], 1.0)
            link(memset(m_pad[:, :], 0.0))
            dve.wait_ge(s["consts_ready"], 4)
            link(dve.tensor_copy(iota[:, :], iota_i[:, :]))
            def prep(q):
                if q == PREPS - 1:
                    dve.wait_ge(s["head_bias_in"], 16 * 6)
                    for z in range(1, 3):
                        last = dve.tensor_copy(head_bias[:, :, z * HD:(z + 1) * HD], head_bias[:, :, 0:HD])
                    last.then_inc(s["head_bias_ready"], 1)
                dve.wait_ge(s["prep_ps"], q + 1)
                bank = prep_bank(q)
                if q < NB // 4:
                    last = dve.tensor_copy(tiles(ctxT[:, q * GK:(q + 1) * GK]), tiles(bank)[:, :, 0:KEYS])
                else:
                    for c in range(4):
                        n = 4 * q + c
                        src = bank[:, c * P:c * P + rows_of[n]]
                        if n == 16:
                            dst = waT[:, :]
                        elif n < 19:
                            dst = wcT[:, n - 17, :]
                        elif n < 31:
                            i, m = divmod(n - 19, 4)
                            dst = (wq[i], wk[i], wvT[i], woT[i])[m][:, :]
                            if m < 2:
                                dst = dst.rearrange("p (h c) -> p h c", c=ROW)[:, :, 0:3 * HD].rearrange("p h (z c) -> p h z c", z=3)
                                src = src.rearrange("p (h c) -> p h c", c=HD)
                                if m == 1:
                                    dve.tensor_scalar(dst[:, :, 1:3], src.unsqueeze(2).broadcast_to([P, H, 2, HD]), -1.0, None, ALU.mult)
                                    dst = dst[:, :, 0]
                                else:
                                    src = src.unsqueeze(2).broadcast_to([P, H, 3, HD])
                        elif n < 39:
                            dst = geT[:, (n - 31) * P:(n - 30) * P]
                        elif n < 47:
                            dst = upT[:, (n - 39) * P:(n - 38) * P]
                        elif n < 49:
                            dst = geT[:, (n - 47 + 8) * P:(n - 46 + 8) * P]
                        elif n < 51:
                            dst = upT[:, (n - 49 + 8) * P:(n - 48 + 8) * P]
                        elif n < 61:
                            dst = dnT[:, n - 51, :]
                        elif n == 61:
                            dve.tensor_copy(r3[:, :], src[:, E16 + 1:])
                            dst, src = r1[:, :], src[:, 0:E16 + 1]
                        elif n == 62:
                            dst = bqk[:, :, :]
                            src = src.rearrange("p (n j) -> p n j", j=NJ)
                        else:
                            dst = b1T[:, :]
                        last = dve.tensor_copy(dst, src)
                last.then_inc(s["prep_sb"], 1)

            def window_tables():
                dve.wait_ge(s["cond_in"], 16 * COND_DMAS)
                link(dve.tensor_copy(lens[:, :], lens_i[:, :]))
                dve.tensor_scalar(w_lo[:, :], pt[:, :], -WINDOW, 0.0, ALU.add, ALU.max)
                link(dve.tensor_scalar(w_hi[:, :], pt[:, :], WINDOW, None, ALU.add))
                link(dve.tensor_tensor(w_hi[:, :], w_hi[:, :], lens[:, :], ALU.min))
                dve.wait_ge(s["x_in"], 16)

            def tables():
                dve.wait_ge(s["prep_sb"], PREPS)
                dve.wait_ge(s["small_in"], 16 * SMALL_DMAS)
                dve.wait_ge(s["pool_step"], 8)
                dve.reduce_sum(q_is_lo[:, :], row_of[:, 2 * HD:3 * HD], AX_X)
                dve.reduce_sum(k_is_lo[:, :], row_of[:, HD:2 * HD], AX_X)
                dve.reduce_sum(k_sign[:, :], row_of[:, HD:3 * HD], AX_X)
                link(dve.tensor_tensor(q_special[:, :], row_of[:, D_ROW:D_ROW + 1], row_of[:, D_ROW + 1:D_ROW + 2], ALU.subtract))
                dve.tensor_tensor(k_is_lo[:, :], k_is_lo[:, :], row_of[:, D_ROW + 1:D_ROW + 2], ALU.add)
                link(dve.tensor_scalar(k_sign[:, :], k_sign[:, :], -2.0, 1.0, ALU.mult, ALU.add))
                for i in range(3):
                    for j in range(NJ):
                        dve.tensor_scalar(q_bias[i][:, j, :], tau[:, :], bqk[:, 2 * i, j:j + 1], q_special[:, 0:1], ALU.mult, ALU.add)
                    last = dve.scalar_tensor_tensor(k_bias[i][:, :], bqk[:, 2 * i + 1, :], k_sign[:, 0:1], row_of[:, M_ROW:M_ROW + NJ], ALU.mult, ALU.add)
                link(last)


            def layer_norm(n, src, dst, done=None, scale=None):
                for b in range(GB):
                    last = dve.bn_stats(stats[:, b, :], src(b))
                link(last, alone=True)
                for b in range(GB):
                    last = dve.bn_aggr(mv[:, b, :], stats[:, b, :])
                last.then_inc(s["ln_var"], 1)
                dve.wait_ge(s["ln_rstd"], n + 1)
                r = rstd
                if scale is not None:
                    link(dve.tensor_tensor(rstd_t[:], rstd[:], scale, ALU.mult))
                    r = rstd_t
                for b in range(GB):
                    last = dve.tensor_scalar(tok(dst, b), src(b), mv[:, b, 0:1], r[:, b:b + 1], ALU.subtract, ALU.mult)
                if done:
                    last.then_inc(s[done], 1)
                else:
                    link(last)

            def bcast(small2d, n):
                return small2d.unsqueeze(2).broadcast_to([small2d.shape[0], small2d.shape[1], n])

            def over(ap2d, n):
                return ap2d.unsqueeze(1).broadcast_to([ap2d.shape[0], n, ap2d.shape[1]])

            def window(i, g, part):
                n = g + 1
                keep, gauss, sc, pen = tmp[:, 0:GK], tmp2[:, 0:GK], probs[:, 0:GK], probs[:, 512:512 + GK]
                pos = over(iota[:, 0:KEYS], GB)
                grp = bass.ds(g * GB, GB)
                if part[0] == "norm":
                    layer_norm(attention_norm(i, g), lambda b: x_tile(g, b), xw, done="xa_ready")
                elif part[0] == "scores":
                    dve.tensor_tensor(tiles(keep), pos, bcast(w_lo[:, grp], KEYS), ALU.is_ge)
                    link(dve.tensor_tensor(tiles(gauss), pos, bcast(w_hi[:, grp], KEYS), ALU.is_le))
                    link(dve.tensor_tensor(keep, keep, gauss, ALU.mult))
                    link(dve.tensor_tensor(tiles(gauss), pos, bcast(pt[:, grp], KEYS), ALU.subtract))
                    dve.tensor_tensor(gauss, gauss, gauss, ALU.mult).then_inc(s["gauss_arg"], 1)
                    link(dve.tensor_scalar(pen, keep, MASKED, -MASKED, ALU.mult, ALU.add))
                    dve.wait_ge(s["score_ps"], n)
                    link(dve.tensor_tensor(sc, psS[:, 1, 0:GK], keep, ALU.mult))
                    link(dve.tensor_tensor(sc, sc, pen, ALU.add))
                    link(dve.reduce_max(top[:, :], tiles(sc), AX_X))
                    dve.tensor_tensor(tiles(sc), tiles(sc), bcast(top[:, :], KEYS), ALU.subtract).then_inc(s["x0_shifted"], 1)
                    dve.wait_ge(s["x0_exp_ready"], n)
                    link(dve.reduce_sum(den[:, :], tiles(sc), AX_X))
                    link(dve.reciprocal(inv[:, :], den[:, :]))
                    dve.wait_ge(s["gauss_ready"], n)
                    for b in range(GB):
                        last = dve.scalar_tensor_tensor(tiles(sc)[:, b, :], tiles(sc)[:, b, :], inv[:, b:b + 1],
                                                        tiles(gauss)[:, b, :], ALU.mult, ALU.mult)
                    last.then_inc(s["align_ready"], 1)
                elif part[0] == "mix":
                    dve.wait_ge(s["tanh_ready"], n)
                    link(dve.tensor_tensor(x_group(g), x_group(g), tmp[:, :], ALU.add), alone=True)

            def parts_of(parts, values, hi, is_lo):
                link(dve.tensor_scalar(hi.bitcast(I32), values.bitcast(I32), HI_MASK, None, ALU.bitwise_and))
                return dve.scalar_tensor_tensor(parts, values, is_lo[:, 0:1], hi, ALU.mult, ALU.subtract)

            def heads(i, g, part):
                a = (i - 1) * NG + g
                w = i - 1
                grp = bass.ds(g * GB, GB)
                if part[0] == "norm":
                    layer_norm(attention_norm(i, g), lambda b: x_tile(g, b), attn, done="xa_ready", scale=tau[:, grp])
                elif part[0] == "keys_read":
                    j = part[1]
                    dve.wait_ge(s["k_ps"], a * NJ + j + 1)
                    k, hi = ks[:, j, :], probs[:, (j % 2) * GT:(j % 2) * GT + GK]
                    dve.scalar_tensor_tensor(k, psS[:, j, 0:GK], k_bias[w][:, j:j + 1], deltaK[:, bass.ds(g * GK, GK)],
                                             ALU.add, ALU.add).then_inc(s["k_read"], 1)
                    dve.wait_ge(s["k_read"], a * NJ + j + 1)
                    if j >= 2:
                        dve.wait_ge(s["k_ready"], a * NJ + j - 1)
                    parts_of(k, k, hi, k_is_lo).then_inc(s["k_ready"], 1)
                elif part[0] == "values":
                    dve.wait_ge(s["v_ps"], a + 1)
                    for b in range(GB):
                        last = dve.tensor_tensor(vaug[:, b, :, 0:HD], psM[0:KEYS, b * P:(b + 1) * P].rearrange("p (h c) -> p h c", c=HD),
                                                 bv[w][0:KEYS, :].rearrange("p (h c) -> p h c", c=HD), ALU.add)
                    last.then_inc(s["v_ready"], 1)
                elif part[0] == "queries":
                    j = part[1]
                    if j == 0:
                        dve.wait_ge(s["k_ready"], a * NJ + NJ)
                    elif j >= 2:
                        dve.wait_ge(s["q_ready"], a * NJ + j - 1)
                    dve.wait_ge(s["q_ps"], a * NJ + j + 1)
                    q, hi = probs[:, j * GT:(j + 1) * GT], (attn, attnT)[j % 2][:, :]
                    dve.tensor_tensor(tiles(q), tiles(psS[:, j, :]), bcast(q_bias[w][:, j, grp], P), ALU.add).then_inc(s["q_read"], 1)
                    dve.wait_ge(s["q_read"], a * NJ + j + 1)
                    parts_of(qs[:, j, :], q, hi, q_is_lo).then_inc(s["q_ready"], 1)
                elif part[0] == "maxima":
                    dve.wait_ge(s["a_ps"], a * GB + part[1] + 1)
                    m_out = m_pad[:, :].rearrange("p (r c) -> p c r", c=ROW)[:, M_ROW:M_ROW + NJ, :]
                    dve.reduce_max(m_out, psS[:, :, 0:GK].rearrange("p j (r k) -> p j r k", k=KEYS), AX_X).then_inc(s["max_ready"], 1)
                elif part[0] == "shift":
                    b = part[1]
                    dve.wait_ge(s["maxT_ps"], a * GB + b + 1)
                    dve.tensor_tensor(tiles(q_shift), qs[:, :, b * P:(b + 1) * P].bitcast(F32), over(psM[:, 0:P], NJ),
                                      ALU.add).then_inc(s["q_shifted"], 1)
                elif part[0] == "divide":
                    b = part[1]
                    dve.wait_ge(s["on_ps"], a * GB + b + 1)
                    ob = psM[:, :].rearrange("p (h c) -> p h c", c=ROW)
                    link(dve.reciprocal(rden[:, b, :], ob[:, :, HD]))
                    dve.tensor_tensor(tok(attn, b).rearrange("p (h c) -> p h c", c=HD), ob[:, :, 0:HD], bcast(rden[:, b, :], HD),
                                      ALU.mult).then_inc(s["attn_ready"], 1)
                elif part[0] == "project":
                    dve.wait_ge(s["wo_ps"], a + 1)
                    dve.tensor_tensor(x_group(g), x_group(g), psS[:, 0, :], ALU.add).then_inc(s["x_done"], 1)
                    dve.wait_ge(s["x_done"], a + 1)
                    link(dve.tensor_tensor(tiles(x_group(g)), tiles(x_group(g)), over(bo[w][:, :], GB), ALU.add), alone=True)

            def route(f, n_e, width, bias):
                dve.wait_ge(s["logits_ps"], f + 1)
                ps = psM[:, 0:GB * width].rearrange("p (b e) -> p b e", e=width)
                if bias is None:
                    link(dve.tensor_copy(lg[:, :, 0:width], ps), alone=True)
                else:
                    link(dve.tensor_tensor(lg[:, :, 0:width], ps, over(bias[:, :], GB), ALU.add), alone=True)
                for b in range(GB):
                    last = dve.max(mx[:, b, :], lg[:, b, 0:n_e])
                link(last)
                dve.tensor_tensor(gap[:, :], mx[:, :, 0], mx[:, :, 1], ALU.subtract).then_inc(s["gap_ready"], 1)
                for b in range(GB):
                    last = dve.max_index(ix[:, b, :], mx[:, b, :], lg[:, b, 0:n_e])
                link(last)
                link(dve.tensor_copy(ixf[:, :, :], ix[:, :, 0:2]))
                pos = over(iota[:, 0:n_e], GB)
                first, second = oh1[:, :, 0:n_e], oh2[:, :, 0:n_e]
                dve.tensor_tensor(first, pos, bcast(ixf[:, :, 0], n_e), ALU.is_equal)
                dve.tensor_tensor(second, pos, bcast(ixf[:, :, 1], n_e), ALU.is_equal)

            def weights(f, n_e, width):
                first, second = oh1[:, :, 0:n_e], oh2[:, :, 0:n_e]
                dve.wait_ge(s["gate_ready"], f + 1)
                dve.tensor_scalar(w1[:, :], th[:, :], 0.5, 0.5, ALU.mult, ALU.add)
                link(dve.tensor_scalar(w2[:, :], th[:, :], -0.5, 0.5, ALU.mult, ALU.add))
                dve.tensor_tensor(first, first, bcast(w1[:, :], n_e), ALU.mult)
                link(dve.tensor_tensor(second, second, bcast(w2[:, :], n_e), ALU.mult))
                if width > n_e:
                    dve.tensor_scalar(comb[:, :, n_e], ths[:, :], 0.5, 0.5, ALU.mult, ALU.add)
                dve.tensor_tensor(comb[:, :, 0:n_e], first, second, ALU.add).then_inc(s["comb_ready"], 1)

            def moe(i, g, part):
                f, m = i * NG + g, MOE_OF[i] * NG + g
                acc = (lambda b: tok(xn, b)) if i == 0 else (lambda b: x_tile(g, b))
                acc_all = xn[:, :] if i == 0 else x_group(g)
                if part[0] == "logits":
                    route(f, E8, E8, {0: rb0, 2: rb2}.get(i))
                elif part[0] == "gate":
                    weights(f, E8, E8)
                elif part[0] == "b2":
                    if i < 3:
                        bm = (m if i == 0 else NG + g) + 1
                        dve.wait_ge(s["b2_ps"], bm)
                        dve.tensor_tensor(acc_all, xa[:, :] if i == 0 else acc_all, psY[:, :], ALU.add).then_inc(s["b2_added"], 1)
                        wait_alone(s["b2_added"], bm)
                elif part[0] == "out":
                    e = part[1]
                    if e:
                        dve.wait_ge(s["y_added"], m * E8 + e)
                    dve.wait_ge(s["y_ps"], m * E8 + e + 1)
                    for b in range(GB):
                        last = dve.scalar_tensor_tensor(acc(b), tok(psY, b), comb[:, b, e:e + 1], acc(b), ALU.mult, ALU.add)
                    last.then_inc(s["y_added"], 1)
                elif part[0] == "end":
                    dve.wait_ge(s["y_added"], m * E8 + E8)
                    if i == 0:
                        layer_norm(LN_BASE[i] + LN_PER[i] * g + 2, lambda b: tok(xn, b), xn)
                        link(dve.tensor_tensor(tiles(xn[:, :]), tiles(xn[:, :]), over(gamma[:, :], GB), ALU.mult))
                        link(dve.tensor_tensor(tiles(xn[:, :]), tiles(xn[:, :]), over(beta[:, :], GB), ALU.add))
                        link(dve.tensor_tensor(x_group(g), x_group(g), xn[:, :], ALU.add))

            def gated(i, g, part):
                if part[0] == "logits":
                    route(NG + g, E16, E16 + 1, None)
                elif part[0] == "gate":
                    weights(NG + g, E16, E16 + 1)
                elif part[0] == "weigh":
                    c = part[1]
                    n = g * CH1 + c
                    dve.wait_ge(s["silu_ready"], n + 1)
                    dve.wait_ge(s["f1_up_ps"], n + 1)
                    dve.tensor_tensor(hT[c % 2][:, 1, :], hT[c % 2][:, 0, :], psH[:, 1, :], ALU.mult).then_inc(s["f1_t_ready"], 1)
                    dve.wait_ge(s["f1_t_ready"], n + 1)
                    dve.wait_ge(s["f1_w_ps"], n + 1)
                    if c >= 2:
                        dve.wait_ge(s["f1_down"], n - 1)
                    dve.tensor_tensor(hT[c % 2][:, 2, :], hT[c % 2][:, 1, :], psH[:, 0, :], ALU.mult).then_inc(s["f1_h_ready"], 1)
                elif part[0] == "end":
                    dve.wait_ge(s["f1_y_ps"], g + 1)
                    link(dve.tensor_tensor(x_group(g), x_group(g), psY[:, :], ALU.add))

            def ahead(i, g, part):
                if part[0] == "norm":
                    layer_norm(experts_norm(i, g), lambda b: x_tile(g, b), xa, done="xn_ready")

            for what, kind, g in steps(dve, window, heads, moe, gated, ahead):
                if what == "prep":
                    prep(g)
                elif what == "window_tables":
                    window_tables()
                elif what == "tables":
                    tables()
                elif what == "end":
                    assert chain["n"] == LINKS[kind], (kind, chain["n"])
                    chain["base"] += (NG - 1) * LINKS[kind]
                    chain["n"], chain["per"], chain["g"] = 0, 0, 0
                else:
                    chain["base"] += chain["n"]
                    chain["n"] = 0
                    if what == "begin":
                        chain["per"], chain["g"] = LINKS[kind], g

        @block.tensor
        def _(pe):
            pe.wait_ge(s["consts_ready"], 4)
            pe.wait_ge(s["ctx_in"], 16 * CTX_DMAS)

            def prep(q):
                if q == NB // 4:
                    pe.wait_ge(s["window_in"], 16 * WINDOW_DMAS)
                elif q == NB // 4 + 1:
                    pe.wait_ge(s["nat_in"], 16 * NAT_DMAS)
                elif q == PREPS - 1:
                    pe.wait_ge(s["head_bias_ready"], 1)
                if prep_before(q):
                    pe.wait_ge(s["prep_sb"], prep_before(q))
                for c in range(4):
                    n = 4 * q + c
                    rows = rows_of[n]
                    last = pe.transpose(prep_bank(q)[:, c * P:c * P + rows], nat[0:rows, n, :], ident[0:rows, 0:rows])
                last.then_inc(s["prep_ps"], 1)

            def mm(o, l, r, start=True, stop=True, **kw):
                return pe.matmul(o, l, r, start=start, stop=stop, **kw)

            def window(i, g, part):
                n = g + 1
                if part[0] == "scores":
                    mm(psS[:, 0, 0:GK], waT[:, :], ctxT[:, bass.ds(g * GK, GK)]).then_inc(s["wa_ps"], 1)
                    pe.wait_ge(s["xa_ready"], n)
                    for b in range(GB):
                        last = pe.transpose(tok(psM, b), tok(xw, b), ident[:, :])
                    last.then_inc(s["xaT_ps"], 1)
                    pe.wait_ge(s["wa_ready"], n)
                    pe.wait_ge(s["xaT_ready"], n)
                    for b in range(GB):
                        last = mm(psS[:, 1, b * KEYS:(b + 1) * KEYS], tok(xaT, b), attn[:, b * KEYS:(b + 1) * KEYS])
                    last.then_inc(s["score_ps"], 1)
                elif part[0] == "align":
                    pe.wait_ge(s["align_ready"], n)
                    for b in range(GB):
                        last = pe.transpose(psM[0:KEYS, b * P:(b + 1) * P], probs[:, b * KEYS:(b + 1) * KEYS], ident[:, :])
                    last.then_inc(s["alignT_ps"], 1)
                elif part[0] == "context":
                    pe.wait_ge(s["alignT_ready"], n)
                    pe.wait_ge(s["ctx_g_in"], n * 16)
                    for b in range(GB):
                        last = mm(psS[:, 2, b * P:(b + 1) * P], ctx_g[:, b, :], probs[0:KEYS, 1024 + b * P:1024 + (b + 1) * P])
                    last.then_inc(s["context_ps"], 1)
                elif part[0] == "mix":
                    pe.wait_ge(s["context_ready"], n)
                    for b in range(GB):
                        mm(psS[:, 3, b * P:(b + 1) * P], tok(attnT, b), wcT[:, 0, :], stop=False)
                        last = mm(psS[:, 3, b * P:(b + 1) * P], tok(xaT, b), wcT[:, 1, :], start=False)
                    last.then_inc(s["mix_ps"], 1)

            def heads(i, g, part):
                w = i - 1
                a = w * NG + g
                if part[0] == "front":
                    pe.wait_ge(s["xa_ready"], i * NG + g + 1)
                    for b in range(GB):
                        last = pe.transpose(tok(psM, b), tok(attn, b), ident[:, :])
                    last.then_inc(s["xaT_ps"], 1)
                elif part[0] == "keys":
                    for j in range(NJ):
                        mm(psS[:, j, 0:GK], wk[w][:, j * P:(j + 1) * P], ctxT[:, bass.ds(g * GK, GK)]).then_inc(s["k_ps"], 1)
                elif part[0] == "values":
                    pe.wait_ge(s["xaT_ready"], i * NG + g + 1)
                    pe.wait_ge(s["ctxT_g_in"], a * 16 + 16)
                    for b in range(GB):
                        last = mm(psM[0:KEYS, b * P:(b + 1) * P], ctxT_g[:, b * KEYS:(b + 1) * KEYS], wvT[w][:, :])
                    last.then_inc(s["v_ps"], 1)
                elif part[0] == "queries":
                    j = part[1]
                    pe.wait_ge(s["k_read"], a * NJ + j + 1)
                    mm(psS[:, j, :], wq[w][:, j * P:(j + 1) * P], xaT[:, :]).then_inc(s["q_ps"], 1)
                elif part[0] == "maxima":
                    b = part[1]
                    if b:
                        pe.wait_ge(s["probs_ready"], a * GB + b)
                    else:
                        pe.wait_ge(s["q_ready"], a * NJ + NJ)
                        pe.wait_ge(s["v_ready"], a + 1)
                    pe.wait_ge(s["kbd_ready"], a * GB + b + 1)
                    for j in range(NJ):
                        last = mm(psS[:, j, 0:GK], qs[:, j, b * P:(b + 1) * P], kbd[:, b % 2, j].rearrange("p r k -> p (r k)"))
                    last.then_inc(s["a_ps"], 1)
                elif part[0] == "shift":
                    b = part[1]
                    pe.wait_ge(s["max_ready"], a * GB + b + 1)
                    if b:
                        pe.wait_ge(s["attn_ready"], a * GB + b)
                    pe.transpose(psM[:, 0:P], m_pad[:, :], ident[:, :]).then_inc(s["maxT_ps"], 1)
                elif part[0] == "scores":
                    b = part[1]
                    pe.wait_ge(s["q_shifted"], a * GB + b + 1)
                    for j in range(NJ):
                        for r in range(4):
                            last = mm(psS[0:KEYS, j, r * P:(r + 1) * P], kbd[:, b % 2, j, r, :].bitcast(F32), q_shift[:, j * P:(j + 1) * P])
                    last.then_inc(s["b_ps"], 1)
                elif part[0] == "output":
                    b = part[1]
                    pe.wait_ge(s["probs_ready"], a * GB + b + 1)
                    for h in range(H):
                        j, r = divmod(h, 4)
                        last = mm(psM[ROW * r:ROW * r + HD + 1, j * P:(j + 1) * P], vaug[:, b, h, :], probs[0:KEYS, h * P:(h + 1) * P])
                    last.then_inc(s["o_ps"], 1)
                elif part[0] == "divide":
                    pe.wait_ge(s["oT_ready"], a * GB + part[1] + 1)
                    for j in range(NJ):
                        last = pe.transpose(tok(psM, j), tok(attnT, j), ident[:, :])
                    last.then_inc(s["on_ps"], 1)
                elif part[0] == "transpose":
                    pe.wait_ge(s["attn_ready"], a * GB + GB)
                    for b in range(GB):
                        last = pe.transpose(tok(psM, b), tok(attn, b), ident[:, :])
                    last.then_inc(s["attnT_ps"], 1)
                elif part[0] == "project":
                    pe.wait_ge(s["attnT_ready"], a + 1)
                    for b in range(GB):
                        last = mm(psS[:, 0, b * P:(b + 1) * P], tok(attnT, b), woT[w][:, :])
                    last.then_inc(s["wo_ps"], 1)

            def ahead(i, g, part):
                if part[0] == "front":
                    pe.wait_ge(s["xn_ready"], i * NG + g + 1)
                    for b in range(GB):
                        last = pe.transpose(tok(psM, b), tok(xa, b), ident[:, :])
                    last.then_inc(s["xnT_ps"], 1)

            def logits(f, router, width):
                pe.wait_ge(s["xnT_ready"], f + 1)
                for b in range(GB):
                    last = mm(psM[:, b * width:(b + 1) * width], tok(xnT, b), router[:, 0:width])
                last.then_inc(s["logits_ps"], 1)

            def comb_transposed(f, width):
                for b in range(GB):
                    last = pe.transpose(psY[0:width, b * P:(b + 1) * P], comb[:, b, 0:width], ident[:, :])
                last.then_inc(s["combT_ps"], 1)

            def moe(i, g, part):
                f, m = i * NG + g, MOE_OF[i] * NG + g
                home = moeB if i == 2 else moeA
                router, b2 = {0: (r0, b2_0), 2: (r2, b2_2), 3: (r3, None)}[i]
                wi, wo = w1_of(home), w2_of(home)
                bm = (g if i == 0 else NG + g) + 1

                def hidden(e, k):
                    c = e * HC + k
                    if c >= 2:
                        pe.wait_ge(s["h_ready"], m * (E8 * HC) + c - 1)
                    mm(psH[:, c % 2, :], wi[:, e * HID + k * P:e * HID + (k + 1) * P], xnT[:, :]).then_inc(s["h_ps"], 1)

                if part[0] == "logits":
                    logits(f, router, E8)
                elif part[0] == "comb":
                    pe.wait_ge(s["comb_ready"], f + 1)
                    if b2 is not None:
                        comb_transposed(f, E8)
                elif part[0] == "b2":
                    if b2 is not None:
                        pe.wait_ge(s["combT_ready"], f + 1)
                        for b in range(GB):
                            last = mm(tok(psY, b), combT[0:E8, b * P:(b + 1) * P], b2[:, :])
                        last.then_inc(s["b2_ps"], 1)
                elif part[0] == "hidden":
                    hidden(part[1], part[2])
                elif part[0] == "out":
                    e = part[1]
                    pe.wait_ge(s["h_ready"], m * (E8 * HC) + (e + 1) * HC)
                    if e:
                        pe.wait_ge(s["y_added"], m * E8 + e)
                    elif b2 is not None:
                        pe.wait_ge(s["b2_added"], bm)
                    for b in range(GB):
                        for k in range(HC):
                            last = mm(tok(psY, b), hT[e % 2][:, k, b * P:(b + 1) * P], wo[:, e, k, :], start=k == 0, stop=k == HC - 1)
                    last.then_inc(s["y_ps"], 1)

            def gated(i, g, part):
                f = i * NG + g
                if part[0] == "logits":
                    logits(f, r1, E16 + 1)
                elif part[0] == "comb":
                    pe.wait_ge(s["comb_ready"], f + 1)
                    comb_transposed(f, E16 + 1)
                    pe.wait_ge(s["combT_ready"], f + 1)
                elif part[0] == "up":
                    c = part[1]
                    if c:
                        pe.wait_ge(s["f1_t_ready"], g * CH1 + c)
                    mm(psH[:, 1, :], upT[:, c * P:(c + 1) * P], xnT[:, :]).then_inc(s["f1_up_ps"], 1)
                elif part[0] == "swish":
                    c = part[1]
                    if c:
                        pe.wait_ge(s["f1_h_ready"], g * CH1 + c)
                    mm(psH[:, 0, :], geT[:, c * P:(c + 1) * P], xnT[:, :]).then_inc(s["f1_ps"], 1)
                elif part[0] == "weigh":
                    c = part[1]
                    pe.wait_ge(s["silu_ready"], g * CH1 + c + 1)
                    mm(psH[:, 0, :], sel[:, c * P:(c + 1) * P], combT[:, :]).then_inc(s["f1_w_ps"], 1)
                elif part[0] == "out":
                    c = part[1]
                    pe.wait_ge(s["f1_h_ready"], g * CH1 + c + 1)
                    mm(psY[:, :], dnT[:, c, :], hT[c % 2][:, 2, :], start=c == 0, stop=c == CH1 - 1).then_inc(s["f1_down"], 1)
                elif part[0] == "end":
                    pe.wait_ge(s["f1_yT_ready"], g + 1)
                    for b in range(GB):
                        last = pe.transpose(tok(psY, b), hT[0][:, 3, b * P:(b + 1) * P], ident[:, :])
                    last.then_inc(s["f1_y_ps"], 1)

            for what, kind, g in steps(pe, window, heads, moe, gated, ahead):
                if what == "prep":
                    prep(g)
                elif what == "window_tables":
                    pe.wait_ge(s["prep_sb"], NB // 4 + 1)
                elif what == "tables":
                    pe.wait_ge(s["prep_sb"], PREPS)
                    pe.wait_ge(s["small_in"], 16 * SMALL_DMAS)
                elif what == "load":
                    home, times = {0: ("moeA_in", 1), 2: ("moeB_in", 1), 3: ("moeA_in", 2)}[g]
                    pe.wait_ge(s[home], times * 16 * MOE_DMAS)


def kernel(**inputs):
    import numpy as _np
    import concourse.bacc as _bacc
    from concourse import mybir as _mybir
    from concourse.bass_utils import run_bass_kernel_spmd as _run

    nc = _bacc.Bacc("TRN2", target_bir_lowering=False, num_devices=1)
    arrays, t = {}, {}
    for name, value in inputs.items():
        a = _np.ascontiguousarray(value)
        arrays[f"in_{name}"] = a
        t[name] = nc.dram_tensor(f"in_{name}", a.shape, _mybir.dt.from_np(a.dtype), kind="ExternalInput").ap()
    out = nc.dram_tensor("out_x", inputs["x"].shape, _mybir.dt.float32, kind="ExternalOutput").ap()
    build(nc, t, out)
    r = _run(nc, [arrays], core_ids=[0])
    return r.results[0]["out_x"]
```
